# Optimizing a Trainium2 kernel written in Bass

```python
import numpy as np
import jax
import jax.numpy as jnp

def _softmax(x, axis=-1):
    return jax.nn.softmax(x, axis=axis)

def _gelu(x):
    return jax.nn.gelu(x, approximate=True)

def _silu(x):
    return jax.nn.silu(x)

def _sigmoid(x):
    return jax.nn.sigmoid(x)

def _layernorm(x, axis=-1, eps=1e-05):
    m = jnp.mean(x, axis=axis, keepdims=True)
    v = jnp.var(x, axis=axis, keepdims=True)
    return (x - m) / jnp.sqrt(v + eps)

def _scatter_add(tgt, idx, src, axis=0):
    return tgt.at[idx].add(src)

def _segment_sum(src, seg, n):
    return jax.ops.segment_sum(src, seg, n)
kernel_name = 'mk_cond_resid_d2_seqx_r2_10f5f1'

def setup_inputs(seed: int=0):
    np.random.seed(seed)
    _w = jnp.asarray

    def _rec_inputs():
        import jax
        import jax.numpy as jnp
        _rk = jax.random.key(seed)
        x = 7.22e-05 + 1 * jax.random.normal(jax.random.fold_in(_rk, 1), (8, 512, 1024), jnp.float32)
        _lenS = 512 - jax.random.randint(jax.random.fold_in(_rk, 7), (8,), 0, max(1, 512 // 4) + 1, jnp.int32)
        _lenS2 = 512 - jax.random.randint(jax.random.fold_in(_rk, 8), (8,), 0, max(1, 512 // 4) + 1, jnp.int32)
        cond_2048 = jax.random.bernoulli(jax.random.fold_in(_rk, 11), 0.8975, (8, 1024)).astype(jnp.float32)
        return (x, cond_2048)
    x, cond_2048 = _rec_inputs()

    def _L0_cond_setup():
        import jax, jax.numpy as jnp
        import numpy as np
        import math
        D_MODEL = 512
        NUM_HEAD = 16
        NEG_INF = -1e+30
        key = jax.random.key(seed)
        k_x, k_m, k_q, k_k, k_v = jax.random.split(key, 5)
        B, C, T = (4, D_MODEL, 1024)
        x = jax.random.normal(k_x, (B, C, T), dtype=jnp.float32)
        mask = (jax.random.uniform(k_m, (B, T)) < 0.9).astype(jnp.float32)
        limit = math.sqrt(6.0 / (C + C))
        Wq = jax.random.uniform(k_q, (C, C), minval=-limit, maxval=limit, dtype=jnp.float32)
        Wk = jax.random.uniform(k_k, (C, C), minval=-limit, maxval=limit, dtype=jnp.float32)
        Wv = jax.random.uniform(k_v, (C, C), minval=-limit, maxval=limit, dtype=jnp.float32)
        b = jnp.zeros((1,), dtype=jnp.float32)
        return {'x': x, 'mask': mask, 'Wq': Wq, 'Wk': Wk, 'Wv': Wv, 'b': b}
    _L0_cond_all = _L0_cond_setup()
    _L0_cond_in = {k: v for k, v in _L0_cond_all.items() if k in ('Wq', 'Wk', 'Wv', 'b')}
    del _L0_cond_all

    def _L1_cond_setup():
        import jax, jax.numpy as jnp
        import numpy as np
        DT = 0.01
        EPSILON = 0.08
        ALPHA = 0.7
        BETA = 0.8
        CLAMP = 20.0
        B, T, N = (128, 128, 1024)

        def _derivative(q, p, drive, coupling, bias):
            i_couple = jnp.tanh(q) @ coupling.T
            dq = q - q ** 3 / 3.0 - p + drive + i_couple + bias
            dp = EPSILON * (q + ALPHA - BETA * p)
            return (dq, dp)

        def _rk4_step(q, p, drive, coupling, bias):
            dq1, dp1 = _derivative(q, p, drive, coupling, bias)
            dq2, dp2 = _derivative(q + 0.5 * DT * dq1, p + 0.5 * DT * dp1, drive, coupling, bias)
            dq3, dp3 = _derivative(q + 0.5 * DT * dq2, p + 0.5 * DT * dp2, drive, coupling, bias)
            dq4, dp4 = _derivative(q + DT * dq3, p + DT * dp3, drive, coupling, bias)
            q_next = q + DT / 6.0 * (dq1 + 2 * dq2 + 2 * dq3 + dq4)
            p_next = p + DT / 6.0 * (dp1 + 2 * dp2 + 2 * dp3 + dp4)
            q_next = jnp.clip(q_next, -CLAMP, CLAMP)
            p_next = jnp.clip(p_next, -CLAMP, CLAMP)
            return (q_next, p_next)
        key = jax.random.key(seed)
        k1, k2, k3, k4 = jax.random.split(key, 4)
        return {'q0': jax.random.normal(k1, (B, N), dtype=jnp.float32), 'p0': jax.random.normal(k2, (B, N), dtype=jnp.float32), 'input_drive_seq': jax.random.normal(k3, (B, T, N), dtype=jnp.float32), 'coupling': jax.random.normal(k4, (N, N), dtype=jnp.float32) * 0.01, 'bias': jnp.zeros((N,), dtype=jnp.float32)}
    _L1_cond_all = _L1_cond_setup()
    _L1_cond_in = {k: v for k, v in _L1_cond_all.items() if k in ('coupling', 'bias')}
    del _L1_cond_all
    return {'x': x, 'cond_2048': cond_2048, 'L0_cond_Wq': _L0_cond_in['Wq'], 'L0_cond_Wk': _L0_cond_in['Wk'], 'L0_cond_Wv': _L0_cond_in['Wv'], 'L0_cond_b': _L0_cond_in['b'], 'L1_cond_coupling': _L1_cond_in['coupling'], 'L1_cond_bias': _L1_cond_in['bias']}

def reference(x, cond_2048, L0_cond_Wq, L0_cond_Wk, L0_cond_Wv, L0_cond_b, L1_cond_coupling, L1_cond_bias):
    import jax
    import jax.numpy as jnp

    def _L0_cond_ref(x, mask, Wq, Wk, Wv, b):
        import jax, jax.numpy as jnp
        import numpy as np
        import math
        D_MODEL = 512
        NUM_HEAD = 16
        NEG_INF = -1e+30
        B, C, T = x.shape
        H = NUM_HEAD
        Dh = C // H

        def proj(W):
            y = jnp.einsum('oc,bct->bto', W, x)
            return y.reshape(B, T, H, Dh).transpose(0, 2, 1, 3)
        Q, K, V = (proj(Wq), proj(Wk), proj(Wv))
        att = jnp.einsum('bhqd,bhkd->bhqk', Q, K) * (1.0 / math.sqrt(Dh))
        att = att + b[0]
        m = mask[:, None, None, :]
        att = att * m + (1.0 - m) * NEG_INF
        att = jax.nn.softmax(att, axis=-1)
        y = jnp.einsum('bhqk,bhkd->bhqd', att, V)
        y = y.transpose(0, 2, 1, 3).reshape(B, T, C)
        return y.transpose(0, 2, 1)

    def _L1_cond_ref(q0, p0, input_drive_seq, coupling, bias):
        import jax, jax.numpy as jnp
        import numpy as np
        DT = 0.01
        EPSILON = 0.08
        ALPHA = 0.7
        BETA = 0.8
        CLAMP = 20.0
        B, T, N = (128, 128, 1024)

        def _derivative(q, p, drive, coupling, bias):
            i_couple = jnp.tanh(q) @ coupling.T
            dq = q - q ** 3 / 3.0 - p + drive + i_couple + bias
            dp = EPSILON * (q + ALPHA - BETA * p)
            return (dq, dp)

        def _rk4_step(q, p, drive, coupling, bias):
            dq1, dp1 = _derivative(q, p, drive, coupling, bias)
            dq2, dp2 = _derivative(q + 0.5 * DT * dq1, p + 0.5 * DT * dp1, drive, coupling, bias)
            dq3, dp3 = _derivative(q + 0.5 * DT * dq2, p + 0.5 * DT * dp2, drive, coupling, bias)
            dq4, dp4 = _derivative(q + DT * dq3, p + DT * dp3, drive, coupling, bias)
            q_next = q + DT / 6.0 * (dq1 + 2 * dq2 + 2 * dq3 + dq4)
            p_next = p + DT / 6.0 * (dp1 + 2 * dp2 + 2 * dp3 + dp4)
            q_next = jnp.clip(q_next, -CLAMP, CLAMP)
            p_next = jnp.clip(p_next, -CLAMP, CLAMP)
            return (q_next, p_next)
        drive_tbn = jnp.swapaxes(input_drive_seq, 0, 1)

        def scan_fn(carry, drive):
            q, p = carry
            q, p = _rk4_step(q, p, drive, coupling, bias)
            return ((q, p), q)
        (_, _), q_trace_tbn = jax.lax.scan(scan_fn, (q0, p0), drive_tbn)
        return jnp.swapaxes(q_trace_tbn, 0, 1)
    x = x + _L0_cond_ref(x, cond_2048, L0_cond_Wq, L0_cond_Wk, L0_cond_Wv, L0_cond_b)
    x = x + _L1_cond_ref(cond_2048, cond_2048, x, L1_cond_coupling, L1_cond_bias)
    return x

_drawn_inputs = setup_inputs


def setup_inputs(seed=0):
    import zlib

    import numpy as np

    out = dict(_drawn_inputs(seed))
    spreads = {'L1_cond_bias': (0.0, 0.1)}
    factors = {}
    for name, (base, spread) in spreads.items():
        noise = np.random.default_rng([zlib.crc32(name.encode()), seed]).standard_normal(out[name].shape)
        drawn = base * np.exp(spread * noise) if base else spread * noise
        out[name] = jnp.asarray(drawn.astype(out[name].dtype))
    for name, factor in factors.items():
        out[name] = (out[name] * factor).astype(out[name].dtype)
    return out
```

```python
from contextlib import ExitStack

import concourse.bass as bass
from concourse import mybir

F32 = mybir.dt.float32
ALU = mybir.AluOpType
ACT = mybir.ActivationFunctionType
AX = mybir.AxisListType

P = 128
QUAD = 32
BANK = 512
NHEAD = 16
NEG_INF = -1e30

FIRST, FIRST_DMA = 1, 16

DT, EPSILON, ALPHA, BETA, CLAMP = 0.01, 0.08, 0.7, 0.8, 20.0


def build_program(nc, x, cond, Wq, Wk, Wv, att_b, coupling, ode_bias, out):
    B, C, N = x.shape
    DH = C // NHEAD
    CC = C // P
    J = N // P
    NH2 = N // BANK
    G = P // QUAD
    JH = J // 2
    STAGES = 4
    SCALE = float(DH) ** -0.5

    q_d = nc.dram_tensor("q_scratch", [B, C, N], F32).ap()
    k_d = nc.dram_tensor("k_scratch", [B, C, N], F32).ap()
    v_d = nc.dram_tensor("v_scratch", [B, NHEAD, P, J * DH], F32).ap()
    xt_d = nc.dram_tensor("xt_scratch", [NHEAD, P, B, J * DH], F32).ap()
    mb_d = nc.dram_tensor("mask_bias_scratch", [B, N], F32).ap()

    with ExitStack() as ctx:
        def sb(name, shape, dt=F32, where=ctx):
            return where.enter_context(nc.sbuf_tensor(name, shape, dt))

        def sem(name):
            return ctx.enter_context(nc.semaphore(name))

        bank = ctx.enter_context(nc.psum_tensor("bank", [P, 8, BANK], F32))
        ident = sb("ident", [P, P])
        cw = sb("cw", [P, J, N])
        bias_col = sb("bias_col", [P, J])
        q0 = sb("q0", [P, J, B])
        p0 = sb("p0", [P, J, B])

        setup(nc, ctx, locals())
        project(nc, ctx, locals())
        attend_and_scan(nc, ctx, locals())


def setup(nc, ctx, e):
    cond, coupling, ode_bias, att_b = e["cond"], e["coupling"], e["ode_bias"], e["att_b"]
    B, C, N, CC, J = e["B"], e["C"], e["N"], e["CC"], e["J"]
    ident, cw, bias_col, q0, p0, bank = e["ident"], e["cw"], e["bias_col"], e["q0"], e["p0"], e["bank"]
    sem = e["sem"]
    id_step, coup_in, small_in, mb_step, mb_out = map(sem, ("id_step", "coup_in", "small_in", "mb_step", "mb_out"))
    group_ready, group_out_a, group_out_v = map(sem, ("setup_group_ready", "setup_out_act", "setup_out_dve"))
    NG = J * J // 4

    with ExitStack() as mem:
        coup = e["sb"]("coup", [P, J, N], F32, mem)
        cond_sb = e["sb"]("cond_sb", [B, N], F32, mem)
        bias_row = e["sb"]("bias_row", [J, P], F32, mem)
        mask_bias = e["sb"]("mask_bias", [B, N], F32, mem)
        inv = e["sb"]("inv", [B, N], F32, mem)
        b_col = e["sb"]("b_col", [B, 1], F32, mem)

        with nc.Block() as block:
            @block.sync
            def _(sp):
                sp.dma_start(cond_sb[:, :], cond).then_inc(small_in, 16)
                sp.dma_start(bias_row[:, :], ode_bias.rearrange("(j p) -> j p", p=P)).then_inc(small_in, 16)
                for b in range(B):
                    sp.dma_start(b_col[b:b + 1, :], att_b.rearrange("(a n) -> a n", a=1)).then_inc(small_in, 16)
                sp.dma_start(coup[:, :, :], coupling.rearrange("(j p) m -> p j m", p=P)).then_inc(coup_in, 16)
                sp.wait_ge(mb_step, 3)
                sp.dma_start(e["mb_d"], mask_bias[:, :]).then_inc(mb_out, 16)
                sp.wait_ge(mb_out, 16)

            @block.gpsimd
            def _(pool):
                nc.gpsimd.memset(ident[:, :], 0.0).then_inc(id_step, 1)
                pool.wait_ge(id_step, 1)
                nc.gpsimd.affine_select(out=ident[:, :], in_=ident[:, :], compare_op=ALU.not_equal, fill=1.0,
                                        base=0, pattern=[[-1, P]], channel_multiplier=1).then_inc(id_step, 1)

            @block.tensor
            def _(pe):
                pe.wait_ge(id_step, 2)
                pe.wait_ge(small_in, 16 * (2 + B))
                for j in range(J):
                    nc.tensor.transpose(bank[:, 0, j * B:(j + 1) * B], cond_sb[:, j * P:(j + 1) * P],
                                        ident[0:B, 0:B])
                nc.tensor.transpose(bank[:, 0, J * B:J * B + J], bias_row[:, :],
                                    ident[0:J, 0:J]).then_inc(group_ready, 1)
                pe.wait_ge(coup_in, 16)
                for g in range(NG):
                    if g >= 7:
                        done = g + 1 - 8
                        pe.wait_ge(group_out_v if done % 2 == 0 else group_out_a, done // 2 + 1)
                    for k in range(4):
                        mj, nj = g // 2, 4 * (g % 2) + k
                        last = nc.tensor.transpose(bank[:, (g + 1) % 8, k * P:(k + 1) * P],
                                                   coup[:, nj, mj * P:(mj + 1) * P], ident[:, :])
                    last.then_inc(group_ready, 1)

            @block.vector
            def _(dve):
                dve.wait_ge(small_in, 16 * (2 + B))
                dve.tensor_scalar(inv[:, :], cond_sb[:, :], -1.0, 1.0, ALU.mult, ALU.add).then_inc(mb_step, 1)
                dve.wait_ge(mb_step, 1)
                dve.tensor_scalar(inv[:, :], inv[:, :], NEG_INF, None, ALU.mult).then_inc(mb_step, 1)
                dve.wait_ge(mb_step, 2)
                dve.scalar_tensor_tensor(mask_bias[:, :], cond_sb[:, :], b_col[:, 0:1], inv[:, :],
                                         ALU.mult, ALU.add).then_inc(mb_step, 1)
                dve.wait_ge(group_ready, 1)
                state = bank[:, 0, 0:J * B].rearrange("p (j b) -> p j b", b=B)
                dve.tensor_copy(q0[:, :, :], state)
                dve.tensor_copy(p0[:, :, :], state)
                dve.tensor_copy(bias_col[:, :], bank[:, 0, J * B:J * B + J]).then_inc(group_out_v, 1)
                for g in range(2, NG + 1, 2):
                    dve.wait_ge(group_ready, g + 1)
                    dve.tensor_copy(cw[:, (g - 1) // 2, (g - 1) % 2 * BANK:((g - 1) % 2 + 1) * BANK],
                                    bank[:, g % 8, :]).then_inc(group_out_v, 1)

            @block.scalar
            def _(act):
                for g in range(1, NG + 1, 2):
                    act.wait_ge(group_ready, g + 1)
                    nc.scalar.copy(cw[:, (g - 1) // 2, (g - 1) % 2 * BANK:((g - 1) % 2 + 1) * BANK],
                                   bank[:, g % 8, :]).then_inc(group_out_a, 1)


def project(nc, ctx, e):
    x, cond, B, C, N, CC, J, DH, SCALE = (e[k] for k in ("x", "cond", "B", "C", "N", "CC", "J", "DH", "SCALE"))
    ident, bank, sem = e["ident"], e["bank"], e["sem"]
    q_d, k_d, v_d, xt_d = e["q_d"], e["k_d"], e["v_d"], e["xt_d"]
    w_in, w_group, w_out = map(sem, ("w_in", "w_group", "w_out"))
    x_in = [sem("x_in0"), sem("x_in1")]
    unit_ready, unit_out_a, unit_out_v = map(sem, ("unit_ready", "unit_out_act", "unit_out_dve"))
    q_saved = [sem("q_saved0"), sem("q_saved1")]
    k_saved = [sem("k_saved0"), sem("k_saved1")]
    v_saved, xt_saved = sem("v_saved"), sem("xt_saved")
    units = [(kind, oc, half) for oc in range(CC) for kind in "qk" for half in range(2)]
    units += [("v", j, 0) for j in range(J)] + [("x", j, 0) for j in range(J)]
    NU = len(units)
    NA = sum(k in "qv" for k, _, _ in units)
    ND = NU - NA
    assert NU % 8 == 0
    a_before = [sum(k in "qv" for k, _, _ in units[:n]) for n in range(NU + 1)]

    with ExitStack() as mem:
        sb = lambda name, shape: e["sb"](name, shape, F32, mem)
        w_nat = sb("w_nat", [P, 3, CC, C])
        w_t = sb("w_t", [P, 3, CC, C])
        xs = sb("xs", [P, 2, CC, N])
        mask_bc = sb("mask_bc", [P, 2, N])
        q_st = sb("q_st", [P, 2, N])
        k_st = sb("k_st", [P, 2, N])
        v_st = sb("v_st", [P, NHEAD, J, DH])
        xt_st = sb("xt_st", [P, NHEAD, J, DH])

        with nc.Block() as block:
            def load_x(sp, par, b):
                sp.dma_start(xs[:, par, :, :], x[b].rearrange("(c p) t -> p c t", p=P)).then_inc(x_in[par], 16)
                sp.dma_start(mask_bc[:, par, :], cond[b].rearrange("(a t) -> a t", a=1).broadcast_to([P, N]))\
                    .then_inc(x_in[par], 16)

            def save_batch(sp, b):
                for oc in range(CC):
                    sp.wait_ge(unit_out_a, FIRST + b * NA + (2 * oc + 2))
                    sp.dma_start(q_d[b, oc * P:(oc + 1) * P, :], q_st[:, oc % 2, :]).then_inc(q_saved[oc % 2], 16)
                    sp.wait_ge(unit_out_v, FIRST + b * ND + (2 * oc + 2))
                    sp.dma_start(k_d[b, oc * P:(oc + 1) * P, :], k_st[:, oc % 2, :]).then_inc(k_saved[oc % 2], 16)
                sp.wait_ge(unit_out_a, FIRST + b * NA + NA)
                sp.dma_start(v_d[b].rearrange("h p x -> p h x"),
                             v_st[:, :, :, :].rearrange("p h j d -> p h (j d)")).then_inc(v_saved, 16)
                sp.wait_ge(unit_out_v, FIRST + b * ND + ND)
                sp.dma_start(xt_d[:, :, b, :].rearrange("h p x -> p h x"),
                             xt_st[:, :, :, :].rearrange("p h j d -> p h (j d)")).then_inc(xt_saved, 16)

            @block.sync
            def _(sp):
                for i, w in enumerate((e["Wq"], e["Wk"], e["Wv"])):
                    sp.dma_start(w_nat[:, i, :, :], w.rearrange("(j p) c -> p j c", p=P)).then_inc(w_in, 16)
                load_x(sp, 0, 0)
                for s in q_saved + k_saved + [v_saved, xt_saved]:
                    sp.sem_inc(s, FIRST_DMA)

                def pair(bp, last):
                    load_x(sp, 1, bp * 2 + 1)
                    save_batch(sp, bp * 2)
                    if not last:
                        load_x(sp, 0, bp * 2 + 2)
                    save_batch(sp, bp * 2 + 1)

                with sp.Fori(0, B // 2 - 1) as bp:
                    pair(bp, False)
                pair(B // 2 - 1, True)
                for s in q_saved + k_saved:
                    sp.wait_ge(s, FIRST_DMA + 16 * B * CC // 2)
                sp.wait_ge(v_saved, FIRST_DMA + 16 * B)
                sp.wait_ge(xt_saved, FIRST_DMA + 16 * B)

            @block.tensor
            def _(pe):
                pe.wait_ge(w_in, 48)
                for i in range(3):
                    for cj in range(CC):
                        g = i * CC + cj
                        if g >= 8:
                            pe.wait_ge(w_out, g - 8 + 1)
                        for oj in range(CC):
                            last = nc.tensor.transpose(bank[:, g % 8, oj * P:(oj + 1) * P],
                                                       w_nat[:, i, oj, cj * P:(cj + 1) * P], ident[:, :])
                        last.then_inc(w_group, 1)
                pe.wait_ge(w_out, 3 * CC)
                with pe.Fori(0, B // 2) as bp:
                    for par in range(2):
                        b = bp * 2 + par
                        pe.wait_ge(x_in[par], bp * 32 + 32)
                        for n, (kind, a, half) in enumerate(units):
                            if n >= 8:
                                old = n - 7
                                pe.wait_ge(unit_out_a, FIRST + b * NA + a_before[old])
                                pe.wait_ge(unit_out_v, FIRST + b * ND + (old - a_before[old]))
                            elif n == 0:
                                pe.wait_ge(unit_out_a, FIRST + b * NA)
                                pe.wait_ge(unit_out_v, FIRST + b * ND)
                            dst = bank[:, n % 8, :]
                            if kind in "qk":
                                for cj in range(CC):
                                    last = nc.tensor.matmul(
                                        dst, w_t[:, "qk".index(kind), cj, a * P:(a + 1) * P],
                                        xs[:, par, cj, half * BANK:(half + 1) * BANK],
                                        start=cj == 0, stop=cj == CC - 1)
                            elif kind == "v":
                                for cj in range(CC):
                                    last = nc.tensor.matmul(dst, xs[:, par, cj, a * P:(a + 1) * P], w_t[:, 2, cj, :],
                                                            start=cj == 0, stop=cj == CC - 1)
                            else:
                                for cj in range(CC):
                                    last = nc.tensor.transpose(dst[:, cj * P:(cj + 1) * P],
                                                               xs[:, par, cj, a * P:(a + 1) * P], ident[:, :])
                            last.then_inc(unit_ready, 1)

            @block.scalar
            def _(act):
                act.sem_inc(unit_out_a, FIRST)
                with act.Fori(0, B // 2) as bp:
                    for par in range(2):
                        b = bp * 2 + par
                        for n, (kind, a, half) in enumerate(units):
                            if kind not in "qv":
                                continue
                            act.wait_ge(unit_ready, b * NU + (n + 1))
                            if kind == "q":
                                if half == 0:
                                    if a >= 2:
                                        act.wait_ge(q_saved[a % 2], FIRST_DMA + b * 32 + 16 * (a // 2))
                                    else:
                                        act.wait_ge(q_saved[a % 2], FIRST_DMA + b * 32)
                                nc.scalar.activation(q_st[:, a % 2, half * BANK:(half + 1) * BANK], bank[:, n % 8, :],
                                                     ACT.Copy, scale=SCALE).then_inc(unit_out_a, 1)
                            else:
                                if a == 0:
                                    act.wait_ge(v_saved, FIRST_DMA + b * 16)
                                nc.scalar.copy(v_st[:, :, a, :], bank[:, n % 8, :].rearrange("p (h d) -> p h d", d=DH))\
                                    .then_inc(unit_out_a, 1)

            @block.vector
            def _(dve):
                for g in range(3 * CC):
                    dve.wait_ge(w_group, g + 1)
                    dve.tensor_copy(w_t[:, g // CC, g % CC, :], bank[:, g % 8, :]).then_inc(w_out, 1)
                dve.sem_inc(unit_out_v, FIRST)
                with dve.Fori(0, B // 2) as bp:
                    for par in range(2):
                        b = bp * 2 + par
                        dve.wait_ge(x_in[par], bp * 32 + 32)
                        for n, (kind, a, half) in enumerate(units):
                            if kind not in "kx":
                                continue
                            dve.wait_ge(unit_ready, b * NU + (n + 1))
                            if kind == "k":
                                if half == 0:
                                    if a >= 2:
                                        dve.wait_ge(k_saved[a % 2], FIRST_DMA + b * 32 + 16 * (a // 2))
                                    else:
                                        dve.wait_ge(k_saved[a % 2], FIRST_DMA + b * 32)
                                cols = slice(half * BANK, (half + 1) * BANK)
                                dve.tensor_tensor(k_st[:, a % 2, cols], bank[:, n % 8, :], mask_bc[:, par, cols],
                                                  ALU.mult).then_inc(unit_out_v, 1)
                            else:
                                if a == 0:
                                    dve.wait_ge(xt_saved, FIRST_DMA + b * 16)
                                dve.tensor_copy(xt_st[:, :, a, :], bank[:, n % 8, :].rearrange("p (h d) -> p h d", d=DH))\
                                    .then_inc(unit_out_v, 1)


def attend_and_scan(nc, ctx, e):
    B, C, N, J, DH, G, JH, STAGES = (e[k] for k in ("B", "C", "N", "J", "DH", "G", "JH", "STAGES"))
    ident, bank, cw, bias_col, q0, p0, sem = (e[k] for k in ("ident", "bank", "cw", "bias_col", "q0", "p0", "sem"))
    q_d, k_d, v_d, xt_d, mb_d, out = (e[k] for k in ("q_d", "k_d", "v_d", "xt_d", "mb_d", "out"))
    QT = N // P
    TILES = 2 * QT
    HALF = 4
    NH = TILES // HALF
    ROUNDS = B // 2

    qkv_in = [sem("qkv_in0"), sem("qkv_in1")]
    xc_in = sem("xc_in")
    pad_ready = sem("pad_ready")
    s_ready, max_ready, exp_done = map(sem, ("s_ready", "max_ready", "exp_done"))
    pt_ready_v, pt_ready_a, pt_out_v, pt_out_a = map(sem, ("pt_ready_v", "pt_ready_a", "pt_out_v", "pt_out_a"))
    o_ready, o_out, ot_ready, ot_red, ot_scaled, recip_ready, head_ready = map(
        sem, ("o_ready", "o_out", "ot_ready", "ot_red", "ot_scaled", "recip_ready", "head_ready"))
    th_a, th_b, main_a, main_b, cp_a, cp_b, tr_a, tr_b, q_a, q_b = map(
        sem, ("th_a", "th_b", "main_a", "main_b", "cp_a", "cp_b", "tr_a", "tr_b", "q_a", "q_b"))
    isum_used, ode_step = sem("isum_used"), sem("ode_step")
    out_t, out_cp_a, out_cp_v, out_saved, drive_ready = map(
        sem, ("out_t", "out_cp_act", "out_cp_dve", "out_saved", "drive_ready"))

    with ExitStack() as mem:
        sb = lambda name, shape: e["sb"](name, shape, F32, mem)
        qp = sb("qp", [P, 2, N])
        kp = sb("kp", [P, 2, N])
        vh = sb("vh", [P, 2, J, DH])
        prob = sb("prob", [P, 2, N])
        prob_t = sb("prob_t", [P, 2, J, BANK])
        nmax = sb("nmax", [P, TILES])
        rsum = sb("rsum", [P, TILES])
        rinv = sb("rinv", [P, TILES])
        o_sb = sb("o_sb", [P, BANK])
        o_red = sb("o_red", [P, HALF, DH])
        o_nrm = sb("o_nrm", [P, HALF, DH])
        xc = sb("xc", [P, B, J, DH])
        xo = sb("xo", [P, J, B, DH])
        drive = sb("drive", [P, B, J, DH])
        th = sb("th", [P, J, B])
        isum = sb("isum", [P, 2, P])
        qs, pst, sq, w3, dmp, ff, base, kk, acc, racc, rr, p0c = (
            sb(n, [P, J, B]) for n in ("qs", "pst", "sq", "w3", "dmp", "ff", "base", "kk", "acc", "racc", "rr", "p0c"))
        outs = sb("outs", [P, 2, J, P])

        S_BANKS = lambda t: bank[:, 2 * (t % 2):2 * (t % 2) + 2, :]
        PT_V, PT_A, O_BANK, OT_BANK = 4, 5, 6, 7
        ac = bank[:, 0:2, 0:P]
        tp = bank[:, 2:4, 0:P]

        with nc.Block() as block:
            @block.sync
            def _(sp):
                sp.sem_inc(out_saved, FIRST_DMA)
                sp.wait_ge(pad_ready, 3)
                with sp.Fori(0, NHEAD) as h:
                    sp.wait_ge(out_saved, FIRST_DMA + h * 128)
                    sp.dma_start(xc[:, :, :, :].rearrange("p b j d -> p b (j d)"), xt_d[h]).then_inc(xc_in, 16)
                    with sp.Fori(0, ROUNDS) as rb:
                        rnd = h * ROUNDS + rb
                        for par in range(2):
                            b = rb * 2 + par
                            sp.wait_ge(o_ready, FIRST + rnd * NH)
                            row = h * DH
                            sp.dma_start(qp[0:DH, par, :], q_d[b, bass.ds(row, DH), :]).then_inc(qkv_in[par], 16)
                            sp.dma_start(kp[0:DH, par, :], k_d[b, bass.ds(row, DH), :]).then_inc(qkv_in[par], 16)
                            sp.dma_start(kp[DH:DH + 1, par, :], mb_d[b].rearrange("(a n) -> a n", a=1))\
                                .then_inc(qkv_in[par], 16)
                            sp.dma_start(vh[:, par, :, :].rearrange("p j d -> p (j d)"), v_d[b, h])\
                                .then_inc(qkv_in[par], 16)
                    for bg in range(2):
                        sp.wait_ge(out_cp_a, h * 2 + (bg + 1))
                        sp.wait_ge(out_cp_v, h * 2 + (bg + 1))
                        for b4 in range(4):
                            sp.dma_start(out[bg * 4 + b4, bass.ds(h * DH, DH), :],
                                         outs[b4 * DH:(b4 + 1) * DH, bg, :, :].rearrange("p j i -> p (j i)"))\
                                .then_inc(out_saved, 16)
                sp.wait_ge(out_saved, FIRST_DMA + NHEAD * 128)

            @block.gpsimd
            def _(pool):
                for t, v in ((qp, 0.0), (kp, 0.0)):
                    nc.gpsimd.memset(t[:, :, :], v).then_inc(pad_ready, 1)
                pool.wait_ge(pad_ready, 2)
                nc.gpsimd.memset(qp[DH:DH + 1, :, :], 1.0).then_inc(pad_ready, 1)

            @block.tensor
            def _(pe):
                pe.sem_inc(o_ready, FIRST)
                pe.sem_inc(ot_ready, FIRST)
                pe.wait_ge(pad_ready, 3)

                def attention_round(h, rb):
                    rnd = h * ROUNDS + rb
                    u = rnd * TILES

                    def scores(t):
                        par, qt = t // QT, t % QT
                        if qt == 0:
                            pe.wait_ge(qkv_in[par], rnd * 64 + 64)
                        if t >= 2:
                            pe.wait_ge(exp_done, u + (t - 1))
                        for half in range(2):
                            last = nc.tensor.matmul(S_BANKS(t)[:, half, :], qp[:, par, qt * P:(qt + 1) * P],
                                                    kp[:, par, half * BANK:(half + 1) * BANK], start=True, stop=True)
                        last.then_inc(s_ready, 1)

                    def turn(t):
                        pe.wait_ge(exp_done, u + (t + 1))
                        for which, (pb, out_sem, ready) in enumerate(
                                ((PT_V, pt_out_v, pt_ready_v), (PT_A, pt_out_a, pt_ready_a))):
                            pe.wait_ge(out_sem, FIRST + u + t)
                            for k in range(4):
                                j = 4 * which + k
                                last = nc.tensor.transpose(bank[:, pb, k * P:(k + 1) * P],
                                                           prob[:, t % 2, j * P:(j + 1) * P], ident[:, :])
                            last.then_inc(ready, 1)

                    def values(n):
                        pe.wait_ge(pt_out_v, FIRST + u + HALF * (n + 1))
                        pe.wait_ge(pt_out_a, FIRST + u + HALF * (n + 1))
                        pe.wait_ge(o_out, FIRST + rnd * NH + n)
                        for k in range(2):
                            for g in range(G):
                                j = 2 * g + k
                                last = nc.tensor.matmul(bank[g * QUAD:g * QUAD + DH, O_BANK, :],
                                                        vh[:, HALF * n // QT, j, :], prob_t[:, n % 2, j, :],
                                                        start=k == 0, stop=k == 1)
                        last.then_inc(o_ready, 1)

                    def turn_values(n):
                        pe.wait_ge(o_out, FIRST + rnd * NH + (n + 1))
                        pe.wait_ge(ot_red, FIRST + rnd * NH + n)
                        for k in range(HALF):
                            last = nc.tensor.transpose(bank[:, OT_BANK, k * P:(k + 1) * P],
                                                       o_sb[:, k * P:(k + 1) * P], ident[:, :])
                        last.then_inc(ot_ready, 1)

                    scores(0)
                    for t in range(TILES):
                        if t + 1 < TILES:
                            scores(t + 1)
                        turn(t)
                        if t % HALF == 0 and t:
                            values(t // HALF - 1)
                        if t % HALF == 2 and t > 2:
                            turn_values(t // HALF - 1)
                    values(NH - 1)
                    turn_values(NH - 1)

                def quarter(mh, nh, ks=range(JH)):
                    for k in ks:
                        mj = mh * JH + k
                        for g in range(G):
                            n0 = nh * BANK + g * P
                            last = nc.tensor.matmul(bank[g * QUAD:g * QUAD + B, nh, 0:P], th[:, mj, :],
                                                    cw[:, mj, n0:n0 + P], start=mj == 0, stop=mj == J - 1,
                                                    skip_group_check=True)
                    return last

                def ode_step_products(st):
                    for s in range(STAGES):
                        pe.wait_ge(th_a, st * STAGES + (s + 1))
                        quarter(0, 0)
                        quarter(0, 1)
                        pe.wait_ge(th_b, st * STAGES + (s + 1))
                        quarter(1, 0).then_inc(main_a, 1)
                        quarter(1, 1, range(0, 2))
                        pe.wait_ge(cp_a, st * STAGES + (s + 1))
                        pe.wait_ge(isum_used, FIRST + st * STAGES + s)
                        nc.tensor.transpose(tp[:, 0, :], isum[:, 0, :], ident[:, :]).then_inc(tr_a, 1)
                        quarter(1, 1, range(2, JH)).then_inc(main_b, 1)
                        pe.wait_ge(cp_b, st * STAGES + (s + 1))
                        nc.tensor.transpose(tp[:, 1, :], isum[:, 1, :], ident[:, :]).then_inc(tr_b, 1)

                with pe.Fori(0, NHEAD) as h:
                    with pe.Fori(0, ROUNDS) as rb:
                        attention_round(h, rb)
                    with pe.Fori(0, DH) as i:
                        ode_step_products(h * DH + i)
                    pe.wait_ge(drive_ready, h * 2 + 2)
                    for n in range(4):
                        bg, nh = n // 2, n % 2
                        for k in range(JH):
                            last = nc.tensor.transpose(
                                bank[:, 4 + n, k * P:(k + 1) * P],
                                xo[:, nh * JH + k, 4 * bg:4 * bg + 4, :].rearrange("p b d -> p (b d)"), ident[:, :])
                        last.then_inc(out_t, 1)
                    pe.wait_ge(out_cp_a, h * 2 + 2)
                    pe.wait_ge(out_cp_v, h * 2 + 2)

            @block.scalar
            def _(act):
                def attention_round(h, rb):
                    rnd = h * ROUNDS + rb
                    u = rnd * TILES

                    def exponent(t):
                        act.wait_ge(max_ready, u + (t + 1))
                        if t >= 2:
                            act.wait_ge(pt_ready_a, u + (t - 1))
                        nc.scalar.activation(prob[:, t % 2, :].rearrange("p (c n) -> p c n", c=2), S_BANKS(t), ACT.Exp,
                                             bias=nmax[:, t:t + 1], scale=1.0,
                                             accum_out=rsum[:, t:t + 1]).then_inc(exp_done, 1)

                    def copy_out(t):
                        n, q = t // HALF, t % HALF
                        act.wait_ge(pt_ready_a, u + (t + 1))
                        if q == 0 and n >= 2:
                            act.wait_ge(o_ready, FIRST + rnd * NH + (n - 1))
                        nc.scalar.copy(prob_t[:, n % 2, 4:8, q * P:(q + 1) * P],
                                       bank[:, PT_A, :].rearrange("p (k n) -> p k n", n=P)).then_inc(pt_out_a, 1)

                    def copy_values(n):
                        act.wait_ge(o_ready, FIRST + rnd * NH + (n + 1))
                        act.wait_ge(ot_ready, FIRST + rnd * NH + n)
                        nc.scalar.copy(o_sb[:, :], bank[:, O_BANK, :]).then_inc(o_out, 1)

                    exponent(0)
                    for t in range(TILES):
                        if t + 1 < TILES:
                            exponent(t + 1)
                        copy_out(t)
                        if t % HALF == 1 and t > 1:
                            copy_values(t // HALF - 1)
                    copy_values(NH - 1)

                def tanh_half(half, done, ready, value):
                    act.wait_ge(done, value)
                    nc.scalar.activation(th[:, half * JH:(half + 1) * JH, :], qs[:, half * JH:(half + 1) * JH, :],
                                         ACT.Tanh).then_inc(ready, 1)

                act.sem_inc(pt_out_a, FIRST)
                act.sem_inc(o_out, FIRST)
                with act.Fori(0, NHEAD) as h:
                    with act.Fori(0, ROUNDS) as rb:
                        attention_round(h, rb)
                    with act.Fori(0, DH) as i:
                        for s in range(STAGES):
                            k = (h * DH + i) * STAGES + s
                            tanh_half(0, q_a, th_a, k + 1)
                            tanh_half(1, q_b, th_b, k + 1)
                            act.wait_ge(main_a, k + 1)
                            nc.scalar.copy(isum[:, 0, :], ac[:, 0, :]).then_inc(cp_a, 1)
                            act.wait_ge(main_b, k + 1)
                            nc.scalar.copy(isum[:, 1, :], ac[:, 1, :]).then_inc(cp_b, 1)
                    for bg in range(2):
                        act.wait_ge(out_t, h * 4 + (2 * bg + 1))
                        nc.scalar.copy(outs[:, bg, 0:JH, :], bank[:, 4 + 2 * bg, :].rearrange("p (j i) -> p j i", i=P))\
                            .then_inc(out_cp_a, 1)

            @block.vector
            def _(dve):
                F = lambda t: t[:, :, :]
                count = [0]
                start = [0]

                def link(ins):
                    count[0] += 1
                    ins.then_inc(ode_step, 1)
                    dve.wait_ge(ode_step, start[0] + count[0])

                def attention_round(h, rb):
                    rnd = h * ROUNDS + rb
                    u = rnd * TILES

                    def row_max(t):
                        dve.wait_ge(s_ready, u + (t + 1))
                        dve.tensor_reduce(nmax[:, t:t + 1], S_BANKS(t), AX.XY, ALU.max, negate=True).then_inc(max_ready, 1)

                    def copy_out(t):
                        n, q = t // HALF, t % HALF
                        dve.wait_ge(pt_ready_v, u + (t + 1))
                        if q == 0 and n >= 2:
                            dve.wait_ge(o_ready, FIRST + rnd * NH + (n - 1))
                        dve.tensor_copy(prob_t[:, n % 2, 0:4, q * P:(q + 1) * P],
                                        bank[:, PT_V, :].rearrange("p (k n) -> p k n", n=P)).then_inc(pt_out_v, 1)

                    def finish(n):
                        dve.reciprocal(rinv[:, HALF * n:HALF * (n + 1)], rsum[:, HALF * n:HALF * (n + 1)])\
                            .then_inc(recip_ready, 1)
                        dve.wait_ge(ot_ready, FIRST + rnd * NH + (n + 1))
                        dve.tensor_reduce(o_red[:, :, :],
                                          bank[:, OT_BANK, :].rearrange("p (q g d) -> p q d g", q=HALF, g=G),
                                          AX.X, ALU.add).then_inc(ot_red, 1)
                        dve.wait_ge(recip_ready, rnd * NH + (n + 1))
                        dve.wait_ge(ot_red, FIRST + rnd * NH + (n + 1))
                        dve.tensor_tensor(o_nrm[:, :, :], o_red[:, :, :],
                                          rinv[:, HALF * n:HALF * (n + 1)].unsqueeze(2).broadcast_to([P, HALF, DH]),
                                          ALU.mult).then_inc(ot_scaled, 1)
                        dve.wait_ge(ot_scaled, rnd * NH + (n + 1))
                        dve.wait_ge(xc_in, h * 16 + 16)
                        q = HALF * n % QT
                        dst = xc[:, rb * 2 + HALF * n // QT, q:q + HALF, :]
                        dve.tensor_tensor(dst, dst, o_nrm[:, :, :], ALU.add).then_inc(head_ready, 1)

                    row_max(0)
                    for t in range(TILES):
                        if t + 1 < TILES:
                            row_max(t + 1)
                        copy_out(t)
                        if t % HALF == 3 and t > 3:
                            finish(t // HALF - 1)
                    finish(NH - 1)

                H = [tp[:, c, :].rearrange("p (g r) -> p g r", r=QUAD)[:, :, 0:B] for c in range(2)]
                TP = tp.rearrange("p c (g r) -> p c g r", r=QUAD)[:, :, :, 0:B]
                halves = lambda t: t[:, :, :].rearrange("p (c g) b -> p c g b", c=2)

                def step(h, i):
                    count[0] = 0
                    st = h * DH + i
                    start[0] = st * PER_STEP
                    D = drive[:, :, :, i].rearrange("p b j -> p j b")
                    dve.wait_ge(drive_ready, h * 2 + 1)
                    for s in range(STAGES):
                        c = (0.5 * DT, 0.5 * DT, DT, DT / 6.0)[s]
                        Q, PP = (q0, p0) if s == 0 else (qs, pst)
                        link(dve.tensor_tensor(F(sq), F(Q), F(Q), ALU.mult))
                        dve.tensor_tensor(F(dmp), D, F(PP), ALU.subtract)
                        link(dve.scalar_tensor_tensor(F(w3), F(sq), -3.0, F(Q), ALU.add, ALU.mult))
                        dve.scalar_tensor_tensor(F(rr), F(PP), -BETA, F(Q), ALU.mult, ALU.add)
                        link(dve.scalar_tensor_tensor(F(ff), F(w3), -1.0 / 3.0, F(dmp), ALU.mult, ALU.add))
                        if s in (0, 2):
                            dve.tensor_scalar(F(p0c), F(p0), c * EPSILON * ALPHA, None, ALU.add)
                        if s < STAGES - 1:
                            link(dve.scalar_tensor_tensor(F(base), F(ff), c, F(q0), ALU.mult, ALU.add))
                            if s == 0:
                                dve.tensor_copy(F(racc), F(rr))
                            else:
                                dve.scalar_tensor_tensor(F(racc), F(rr), 2.0, F(racc), ALU.mult, ALU.add)
                            link(dve.scalar_tensor_tensor(F(pst), F(rr), c * EPSILON, F(p0c), ALU.mult, ALU.add))
                        else:
                            link(dve.tensor_tensor(F(ff), F(ff), F(acc), ALU.add))
                            link(dve.scalar_tensor_tensor(F(base), F(ff), c, F(q0), ALU.mult, ALU.add))
                            link(dve.tensor_tensor(F(racc), F(rr), F(racc), ALU.add))
                            link(dve.scalar_tensor_tensor(F(p0), F(racc), c * EPSILON, F(p0c), ALU.mult, ALU.add))
                            link(dve.tensor_scalar(F(p0), F(p0), -CLAMP, CLAMP, ALU.max, ALU.min))
                        k = st * STAGES + s
                        dve.wait_ge(tr_a, k + 1)
                        dve.scalar_tensor_tensor(qs[:, 0:JH, :], H[0], c, base[:, 0:JH, :], ALU.mult, ALU.add)\
                            .then_inc(q_a, 1)
                        dve.wait_ge(tr_b, k + 1)
                        dve.scalar_tensor_tensor(qs[:, JH:J, :], H[1], c, base[:, JH:J, :], ALU.mult, ALU.add)\
                            .then_inc(q_b, 1)
                        if s < STAGES - 1:
                            dve.tensor_tensor(halves(kk), TP, halves(ff), ALU.add).then_inc(isum_used, 1)
                            dve.wait_ge(q_a, k + 2)
                            dve.wait_ge(q_b, k + 2)
                            dve.wait_ge(isum_used, FIRST + k + 1)
                            if s == 0:
                                link(dve.tensor_copy(F(acc), F(kk)))
                            else:
                                link(dve.scalar_tensor_tensor(F(acc), F(kk), 2.0, F(acc), ALU.mult, ALU.add))
                        else:
                            dve.wait_ge(q_a, k + 2)
                            dve.wait_ge(q_b, k + 2)
                            dve.tensor_scalar(F(q0), F(qs), -CLAMP, CLAMP, ALU.max, ALU.min).then_inc(isum_used, 1)
                            dve.wait_ge(isum_used, FIRST + k + 1)
                            dve.tensor_tensor(xo[:, :, :, i], xc[:, :, :, i].rearrange("p b j -> p j b"),
                                              F(q0), ALU.add).then_inc(ode_step, 1)
                            count[0] += 1
                    return count[0]

                dve.sem_inc(pt_out_v, FIRST)
                dve.sem_inc(ot_red, FIRST)
                dve.sem_inc(isum_used, FIRST)
                dve.tensor_copy(qs[:, 0:JH, :], q0[:, 0:JH, :]).then_inc(q_a, 1)
                dve.tensor_copy(qs[:, JH:J, :], q0[:, JH:J, :]).then_inc(q_b, 1)
                with dve.Fori(0, NHEAD) as h:
                    with dve.Fori(0, ROUNDS) as rb:
                        attention_round(h, rb)
                    dve.wait_ge(head_ready, (h + 1) * (ROUNDS * NH))
                    dve.tensor_tensor(drive[:, :, :, :], xc[:, :, :, :],
                                      bias_col[:, :].unsqueeze(1).unsqueeze(3).broadcast_to([P, B, J, DH]),
                                      ALU.add).then_inc(drive_ready, 1)
                    with dve.Fori(0, DH) as i:
                        made = step(h, i)
                    assert made == PER_STEP, made
                    dve.wait_ge(ode_step, (h + 1) * (DH * PER_STEP))
                    dve.tensor_copy(rr[:, 0:1, 0:1], q0[:, 0:1, 0:1]).then_inc(drive_ready, 1)
                    for bg in range(2):
                        dve.wait_ge(out_t, h * 4 + (2 * bg + 2))
                        dve.tensor_copy(outs[:, bg, JH:J, :], bank[:, 5 + 2 * bg, :].rearrange("p (j i) -> p j i", i=P))\
                            .then_inc(out_cp_v, 1)


PER_STEP = 27


_INS = ["x", "cond_2048", "L0_cond_Wq", "L0_cond_Wk", "L0_cond_Wv", "L0_cond_b", "L1_cond_coupling", "L1_cond_bias"]
_OUTS = [((8, 512, 1024), "float32")]


def kernel(**inputs):
    import numpy as _np
    import concourse.bacc as _bacc
    from concourse import mybir as _mybir
    from concourse.bass_utils import run_bass_kernel_spmd as _run

    nc = _bacc.Bacc("TRN2", target_bir_lowering=False, num_devices=1)
    arrays, args = {}, []
    for name in _INS:
        a = _np.ascontiguousarray(inputs[name])
        arrays[f"in_{name}_dram"] = a
        args.append(nc.dram_tensor(f"in_{name}_dram", a.shape, _mybir.dt.from_np(a.dtype), kind="ExternalInput").ap())
    for i, (shape, dtype) in enumerate(_OUTS):
        dt = _mybir.dt.from_np(_np.dtype(dtype))
        args.append(nc.dram_tensor(f"out_{i}_dram", shape, dt, kind="ExternalOutput").ap())
    build_program(nc, *args)
    r = _run(nc, [arrays], core_ids=[0])
    return r.results[0]["out_0_dram"]
```

```python
from contextlib import ExitStack

import concourse.bass as bass
from concourse import mybir

F32 = mybir.dt.float32
F16 = mybir.dt.float16
BF16 = mybir.dt.bfloat16
I32 = mybir.dt.int32
ALU = mybir.AluOpType
ACT = mybir.ActivationFunctionType
AX = mybir.AxisListType
ALL_MAX = bass.bass_isa.ReduceOp.max

P = 128
QUAD = 32
BANK = 512
NHEAD = 16
NEG_INF = -1e30

FIRST, FIRST_DMA = 1, 16

DT, EPSILON, ALPHA, BETA, CLAMP = 0.01, 0.08, 0.7, 0.8, 20.0
STAGES = 4
STAGE_C = (0.5 * DT, 0.5 * DT, DT, DT / 6.0)

W_EXP = 14
TANH_SCALE = 2.0 ** 11
H_COL, L_COL, M_COLS = 0, 16, 24


def build_program(nc, x, cond, Wq, Wk, Wv, att_b, coupling, ode_bias, out):
    B, C, N = x.shape
    DH = C // NHEAD
    CC = C // P
    J = N // P
    G = P // QUAD
    JH = J // 2
    ELEMENTS = NHEAD * B
    SCALE = float(DH) ** -0.5

    q_d = nc.dram_tensor("q_scratch", [ELEMENTS, 3, DH, N], BF16).ap()
    k_d = nc.dram_tensor("k_scratch", [ELEMENTS, 3, DH, N], BF16).ap()
    v_d = nc.dram_tensor("v_scratch", [ELEMENTS, P, J * DH], F32).ap()
    xt_d = nc.dram_tensor("xt_scratch", [ELEMENTS, P, J * DH], F32).ap()
    x2_d = nc.dram_tensor("x2_scratch", [ELEMENTS, P, J * DH], F32).ap()
    mb_d = nc.dram_tensor("mask_bias_scratch", [B, 3, N], BF16).ap()

    with ExitStack() as ctx:
        def sb(name, shape, dt=F32, where=ctx):
            return where.enter_context(nc.sbuf_tensor(name, shape, dt))

        def sem(name):
            return ctx.enter_context(nc.semaphore(name))

        bank = ctx.enter_context(nc.psum_tensor("bank", [P, 8, BANK], F32))
        ident = sb("ident", [P, P])
        cwh = sb("cwh", [P, 2, J, N], F16)
        isum_c = sb("isum_c", [P, STAGES])
        unscale = sb("unscale", [P, 1])
        bias_col = sb("bias_col", [P, J])
        q0 = sb("q0", [P, J, B])
        p0 = sb("p0", [P, J, B])

        setup(nc, locals())
        project(nc, locals())
        attend_and_scan(nc, locals())


def setup(nc, e):
    cond, coupling, ode_bias, att_b = e["cond"], e["coupling"], e["ode_bias"], e["att_b"]
    B, N, J = e["B"], e["N"], e["J"]
    ident, cwh, bias_col, q0, p0, bank = e["ident"], e["cwh"], e["bias_col"], e["q0"], e["p0"], e["bank"]
    isum_c, unscale = e["isum_c"], e["unscale"]
    sem = e["sem"]
    id_step, coup_in, small_in, mb_step, mb_out = map(sem, ("id_step", "coup_in", "small_in", "mb_step", "mb_out"))
    scale_step, row_max, all_max = map(sem, ("scale_step", "row_max", "all_max"))
    group_ready, state_out, high_out, low_out = map(sem, ("setup_group_ready", "state_out", "high_out", "low_out"))
    NG = J * J // 4

    with ExitStack() as mem:
        coup = e["sb"]("coup", [P, J, N], F32, mem)
        cond_sb = e["sb"]("cond_sb", [B, N], F32, mem)
        bias_row = e["sb"]("bias_row", [J, P], F32, mem)
        mask_bias = e["sb"]("mask_bias", [B, N], F32, mem)
        mask_rest = e["sb"]("mask_rest", [B, N], F32, mem)
        mask_parts = e["sb"]("mask_parts", [B, 3, N], BF16, mem)
        inv = e["sb"]("inv", [B, N], F32, mem)
        b_col = e["sb"]("b_col", [B, 1], F32, mem)
        part_max = e["sb"]("part_max", [P, 1], F32, mem)
        abs_max = e["sb"]("abs_max", [P, 1], F32, mem)
        abs_floor = e["sb"]("abs_floor", [P, 1], F32, mem)
        exponent = e["sb"]("exponent", [P, 1], I32, mem)
        w_scale = e["sb"]("w_scale", [P, 1], I32, mem)

        with nc.Block() as block:
            @block.sync
            def _(sp):
                sp.dma_start(coup[:, :, :], coupling.rearrange("(j p) m -> p j m", p=P)).then_inc(coup_in, 16)
                sp.dma_start(cond_sb[:, :], cond).then_inc(small_in, 16)
                sp.dma_start(bias_row[:, :], ode_bias.rearrange("(j p) -> j p", p=P)).then_inc(small_in, 16)
                sp.dma_start(b_col[:, :], att_b.rearrange("(a n) -> a n", a=1).broadcast_to([B, 1]))\
                    .then_inc(small_in, 16)
                sp.wait_ge(mb_step, 7)
                sp.dma_start(e["mb_d"], mask_parts[:, :, :]).then_inc(mb_out, 16)
                sp.wait_ge(mb_out, 16)

            @block.gpsimd
            def _(pool):
                nc.gpsimd.memset(ident[:, :], 0.0).then_inc(id_step, 1)
                pool.wait_ge(id_step, 1)
                nc.gpsimd.affine_select(out=ident[:, :], in_=ident[:, :], compare_op=ALU.not_equal, fill=1.0,
                                        base=0, pattern=[[-1, P]], channel_multiplier=1).then_inc(id_step, 1)
                pool.wait_ge(row_max, 1)
                nc.gpsimd.partition_all_reduce(abs_max[:, :], part_max[:, :], P, ALL_MAX).then_inc(all_max, 1)

            @block.tensor
            def _(pe):
                pe.wait_ge(id_step, 2)
                pe.wait_ge(small_in, 48)
                for j in range(J):
                    nc.tensor.transpose(bank[:, 0, j * B:(j + 1) * B], cond_sb[:, j * P:(j + 1) * P],
                                        ident[0:B, 0:B])
                nc.tensor.transpose(bank[:, 0, J * B:J * B + J], bias_row[:, :],
                                    ident[0:J, 0:J]).then_inc(group_ready, 1)
                pe.wait_ge(coup_in, 16)
                for g in range(NG):
                    if g == 7:
                        pe.wait_ge(state_out, 1)
                    if g > 7:
                        pe.wait_ge(low_out, g - 7)
                    for k in range(4):
                        mj, nj = g // 2, 4 * (g % 2) + k
                        last = nc.tensor.transpose(bank[:, (g + 1) % 8, k * P:(k + 1) * P],
                                                   coup[:, nj, mj * P:(mj + 1) * P], ident[:, :])
                    last.then_inc(group_ready, 1)

            def w_half(part, g):
                return cwh[:, part, g // 2, g % 2 * BANK:(g % 2 + 1) * BANK]

            @block.vector
            def _(dve):
                dve.wait_ge(small_in, 48)
                dve.tensor_scalar(inv[:, :], cond_sb[:, :], -1.0, 1.0, ALU.mult, ALU.add).then_inc(mb_step, 1)
                dve.wait_ge(mb_step, 1)
                dve.tensor_scalar(inv[:, :], inv[:, :], NEG_INF, None, ALU.mult).then_inc(mb_step, 1)
                dve.wait_ge(mb_step, 2)
                dve.scalar_tensor_tensor(mask_bias[:, :], cond_sb[:, :], b_col[:, 0:1], inv[:, :],
                                         ALU.mult, ALU.add).then_inc(mb_step, 1)
                dve.wait_ge(mb_step, 3)
                dve.tensor_copy(mask_parts[:, 0, :], mask_bias[:, :]).then_inc(mb_step, 1)
                dve.wait_ge(mb_step, 4)
                dve.tensor_tensor(mask_rest[:, :], mask_bias[:, :], mask_parts[:, 0, :], ALU.subtract)\
                    .then_inc(mb_step, 1)
                dve.wait_ge(mb_step, 5)
                dve.tensor_copy(mask_parts[:, 1, :], mask_rest[:, :]).then_inc(mb_step, 1)
                dve.wait_ge(mb_step, 6)
                dve.tensor_tensor(mask_parts[:, 2, :], mask_rest[:, :], mask_parts[:, 1, :], ALU.subtract)\
                    .then_inc(mb_step, 1)

                dve.wait_ge(coup_in, 16)
                dve.tensor_reduce(part_max[:, :], coup[:, :, :], AX.XY, ALU.max, apply_absolute_value=True)\
                    .then_inc(row_max, 1)
                dve.wait_ge(all_max, 1)
                dve.tensor_scalar(abs_floor[:, :], abs_max[:, :], 2.0 ** -100, None, ALU.max).then_inc(scale_step, 1)
                dve.wait_ge(scale_step, 1)
                dve.tensor_scalar(exponent[:, :], abs_floor[:, :].bitcast(I32), 0x7f800000, None, ALU.bitwise_and)\
                    .then_inc(scale_step, 1)
                dve.wait_ge(scale_step, 2)
                dve.tensor_scalar(w_scale[:, :], exponent[:, :], -1.0, float((254 + W_EXP) << 23), ALU.mult, ALU.add)\
                    .then_inc(scale_step, 1)
                undo = 2.0 ** -W_EXP / TANH_SCALE
                for s, c in enumerate(STAGE_C):
                    dve.tensor_scalar(isum_c[:, s:s + 1], exponent[:, :].bitcast(F32), c * undo, None, ALU.mult)
                dve.tensor_scalar(unscale[:, :], exponent[:, :].bitcast(F32), undo, None, ALU.mult)

                dve.wait_ge(group_ready, 1)
                state = bank[:, 0, 0:J * B].rearrange("p (j b) -> p j b", b=B)
                dve.tensor_copy(q0[:, :, :], state)
                dve.tensor_copy(p0[:, :, :], state)
                dve.tensor_copy(bias_col[:, :], bank[:, 0, J * B:J * B + J]).then_inc(state_out, 1)
                dve.wait_ge(scale_step, 3)
                for g in range(NG):
                    dve.wait_ge(high_out, g + 1)
                    dve.scalar_tensor_tensor(w_half(1, g), bank[:, (g + 1) % 8, :], w_scale[:, :].bitcast(F32),
                                             w_half(0, g), ALU.mult, ALU.subtract).then_inc(low_out, 1)

            @block.scalar
            def _(act):
                act.wait_ge(scale_step, 3)
                for g in range(NG):
                    act.wait_ge(group_ready, g + 2)
                    nc.scalar.activation(w_half(0, g), bank[:, (g + 1) % 8, :], ACT.Copy,
                                         scale=w_scale[:, :].bitcast(F32)).then_inc(high_out, 1)


def project(nc, e):
    x, cond, B, C, N, CC, J, DH, SCALE = (e[k] for k in ("x", "cond", "B", "C", "N", "CC", "J", "DH", "SCALE"))
    ident, bank, sem = e["ident"], e["bank"], e["sem"]
    q_d, k_d, v_d, xt_d = e["q_d"], e["k_d"], e["v_d"], e["xt_d"]
    w_in, w_group, w_out = map(sem, ("w_in", "w_group", "w_out"))
    x_in = [sem("x_in0"), sem("x_in1")]
    unit_ready, unit_out_a, unit_out_v = map(sem, ("unit_ready", "unit_out_act", "unit_out_dve"))
    q_saved = [sem("q_saved0"), sem("q_saved1")]
    k_saved = [sem("k_saved0"), sem("k_saved1")]
    part0_ready, rest_ready, part1_ready, part2_ready = map(
        sem, ("part0_ready", "rest_ready", "part1_ready", "part2_ready"))
    v_saved, xt_saved = sem("v_saved"), sem("xt_saved")
    units = [(kind, oc, half) for oc in range(CC) for kind in "qk" for half in range(2)]
    units += [("v", j, 0) for j in range(J)] + [("x", j, 0) for j in range(J)]
    NU = len(units)
    NA = sum(k in "qv" for k, _, _ in units)
    ND = NU - NA
    NQK = sum(k in "qk" for k, _, _ in units)
    assert NU % 8 == 0
    a_before = [sum(k in "qv" for k, _, _ in units[:n]) for n in range(NU + 1)]

    with ExitStack() as mem:
        sb = lambda name, shape: e["sb"](name, shape, F32, mem)
        w_nat = sb("w_nat", [P, 3, CC, C])
        w_t = sb("w_t", [P, 3, CC, C])
        xs = sb("xs", [P, 2, CC, N])
        mask_bc = sb("mask_bc", [P, 2, N])
        st = {k: e["sb"](f"{k}_st", [P, 2, 3, N], BF16, mem) for k in "qk"}
        full = sb("full", [P, 2, BANK])
        rest = sb("rest", [P, 2, BANK])
        v_st = sb("v_st", [P, NHEAD, J, DH])
        xt_st = sb("xt_st", [P, NHEAD, J, DH])

        with nc.Block() as block:
            def load_x(sp, par, b):
                sp.dma_start(xs[:, par, :, :], x[b].rearrange("(c p) t -> p c t", p=P)).then_inc(x_in[par], 16)
                sp.dma_start(mask_bc[:, par, :], cond[b].rearrange("(a t) -> a t", a=1).broadcast_to([P, N]))\
                    .then_inc(x_in[par], 16)

            def save_batch(sp, b):
                for oc in range(CC):
                    for i, (dst, saved) in enumerate(((q_d, q_saved), (k_d, k_saved))):
                        sp.wait_ge(part2_ready, b * NQK + (4 * oc + 2 * i + 2))
                        for part in range(3):
                            sp.dma_start(dst.rearrange("(h b) r d t -> h b r d t", b=B)[4 * oc:4 * oc + 4, b, part, :, :],
                                         st["qk"[i]][:, oc % 2, part, :]).then_inc(saved[oc % 2], 16)
                sp.wait_ge(unit_out_a, FIRST + b * NA + NA)
                sp.dma_start(v_d.rearrange("(h b) p x -> b p h x", b=B)[b],
                             v_st[:, :, :, :].rearrange("p h j d -> p h (j d)")).then_inc(v_saved, 16)
                sp.wait_ge(unit_out_v, FIRST + b * ND + ND)
                sp.dma_start(xt_d.rearrange("(h b) p x -> b p h x", b=B)[b],
                             xt_st[:, :, :, :].rearrange("p h j d -> p h (j d)")).then_inc(xt_saved, 16)

            @block.sync
            def _(sp):
                for i, w in enumerate((e["Wq"], e["Wk"], e["Wv"])):
                    sp.dma_start(w_nat[:, i, :, :], w.rearrange("(j p) c -> p j c", p=P)).then_inc(w_in, 16)
                load_x(sp, 0, 0)
                for s in q_saved + k_saved + [v_saved, xt_saved]:
                    sp.sem_inc(s, FIRST_DMA)

                def pair(bp, last):
                    load_x(sp, 1, bp * 2 + 1)
                    save_batch(sp, bp * 2)
                    if not last:
                        load_x(sp, 0, bp * 2 + 2)
                    save_batch(sp, bp * 2 + 1)

                with sp.Fori(0, B // 2 - 1) as bp:
                    pair(bp, False)
                pair(B // 2 - 1, True)
                for s in q_saved + k_saved:
                    sp.wait_ge(s, FIRST_DMA + 48 * B * CC // 2)
                sp.wait_ge(v_saved, FIRST_DMA + 16 * B)
                sp.wait_ge(xt_saved, FIRST_DMA + 16 * B)

            @block.tensor
            def _(pe):
                pe.wait_ge(w_in, 48)
                for i in range(3):
                    for cj in range(CC):
                        g = i * CC + cj
                        if g >= 8:
                            pe.wait_ge(w_out, g - 8 + 1)
                        for oj in range(CC):
                            last = nc.tensor.transpose(bank[:, g % 8, oj * P:(oj + 1) * P],
                                                       w_nat[:, i, oj, cj * P:(cj + 1) * P], ident[:, :])
                        last.then_inc(w_group, 1)
                pe.wait_ge(w_out, 3 * CC)
                with pe.Fori(0, B // 2) as bp:
                    for par in range(2):
                        b = bp * 2 + par
                        pe.wait_ge(x_in[par], bp * 32 + 32)
                        for n, (kind, a, half) in enumerate(units):
                            if n >= 8:
                                old = n - 7
                                pe.wait_ge(unit_out_a, FIRST + b * NA + a_before[old])
                                pe.wait_ge(unit_out_v, FIRST + b * ND + (old - a_before[old]))
                            elif n == 0:
                                pe.wait_ge(unit_out_a, FIRST + b * NA)
                                pe.wait_ge(unit_out_v, FIRST + b * ND)
                            dst = bank[:, n % 8, :]
                            if kind in "qk":
                                for cj in range(CC):
                                    last = nc.tensor.matmul(
                                        dst, w_t[:, "qk".index(kind), cj, a * P:(a + 1) * P],
                                        xs[:, par, cj, half * BANK:(half + 1) * BANK],
                                        start=cj == 0, stop=cj == CC - 1)
                            elif kind == "v":
                                for cj in range(CC):
                                    last = nc.tensor.matmul(dst, xs[:, par, cj, a * P:(a + 1) * P], w_t[:, 2, cj, :],
                                                            start=cj == 0, stop=cj == CC - 1)
                            else:
                                for cj in range(CC):
                                    last = nc.tensor.transpose(dst[:, cj * P:(cj + 1) * P],
                                                               xs[:, par, cj, a * P:(a + 1) * P], ident[:, :])
                            last.then_inc(unit_ready, 1)

            def split_unit(eng, g, kind, a, half, n, which):
                parity = n % 2
                cols = slice(half * BANK, (half + 1) * BANK)
                parts = st[kind][:, a % 2, :, cols]
                if which == "act":
                    nc.scalar.copy(parts[:, 0, :], full[:, parity, :]).then_inc(part0_ready, 1)
                    eng.wait_ge(rest_ready, g + 1)
                    nc.scalar.copy(parts[:, 1, :], rest[:, parity, :]).then_inc(part1_ready, 1)
                else:
                    eng.wait_ge(part0_ready, g + 1)
                    nc.vector.tensor_tensor(rest[:, parity, :], full[:, parity, :], parts[:, 0, :], ALU.subtract)\
                        .then_inc(rest_ready, 1)
                    eng.wait_ge(part1_ready, g + 1)
                    nc.vector.tensor_tensor(parts[:, 2, :], rest[:, parity, :], parts[:, 1, :], ALU.subtract)\
                        .then_inc(part2_ready, 1)

            @block.scalar
            def _(act):
                act.sem_inc(unit_out_a, FIRST)
                with act.Fori(0, B // 2) as bp:
                    for par in range(2):
                        b = bp * 2 + par
                        for n, (kind, a, half) in enumerate(units):
                            if kind == "x":
                                continue
                            if kind == "v":
                                if a == 0:
                                    act.wait_ge(v_saved, FIRST_DMA + b * 16)
                                act.wait_ge(unit_ready, b * NU + (n + 1))
                                nc.scalar.copy(v_st[:, :, a, :], bank[:, n % 8, :].rearrange("p (h d) -> p h d", d=DH))\
                                    .then_inc(unit_out_a, 1)
                                continue
                            if kind == "q":
                                act.wait_ge(unit_ready, b * NU + (n + 1))
                                nc.scalar.activation(full[:, n % 2, :], bank[:, n % 8, :], ACT.Copy, scale=SCALE)\
                                    .then_inc(unit_out_a, 1)
                            if half == 0:
                                saved = (q_saved if kind == "q" else k_saved)[a % 2]
                                act.wait_ge(saved, FIRST_DMA + b * 96 + 48 * (a // 2))
                            if kind == "q":
                                act.wait_ge(unit_out_a, FIRST + b * NA + a_before[n + 1])
                            else:
                                act.wait_ge(unit_out_v, FIRST + b * ND + (n + 1 - a_before[n + 1]))
                            split_unit(act, b * NQK + n, kind, a, half, n, "act")

            @block.vector
            def _(dve):
                for g in range(3 * CC):
                    dve.wait_ge(w_group, g + 1)
                    dve.tensor_copy(w_t[:, g // CC, g % CC, :], bank[:, g % 8, :]).then_inc(w_out, 1)
                dve.sem_inc(unit_out_v, FIRST)
                with dve.Fori(0, B // 2) as bp:
                    for par in range(2):
                        b = bp * 2 + par
                        for n, (kind, a, half) in enumerate(units):
                            if kind == "v":
                                continue
                            if kind == "x":
                                if a == 0:
                                    dve.wait_ge(xt_saved, FIRST_DMA + b * 16)
                                dve.wait_ge(unit_ready, b * NU + (n + 1))
                                dve.tensor_copy(xt_st[:, :, a, :], bank[:, n % 8, :].rearrange("p (h d) -> p h d", d=DH))\
                                    .then_inc(unit_out_v, 1)
                                continue
                            if kind == "k":
                                if n == 2:
                                    dve.wait_ge(x_in[par], bp * 32 + 32)
                                dve.wait_ge(unit_ready, b * NU + (n + 1))
                                dve.tensor_tensor(full[:, n % 2, :], bank[:, n % 8, :],
                                                  mask_bc[:, par, half * BANK:(half + 1) * BANK], ALU.mult)\
                                    .then_inc(unit_out_v, 1)
                            split_unit(dve, b * NQK + n, kind, a, half, n, "dve")


def attend_and_scan(nc, e):
    B, N, J, DH, G, JH, ELEMENTS = (e[k] for k in ("B", "N", "J", "DH", "G", "JH", "ELEMENTS"))
    ident, bank, cwh, bias_col, q0, p0, sem = (e[k] for k in ("ident", "bank", "cwh", "bias_col", "q0", "p0", "sem"))
    isum_c, unscale = e["isum_c"], e["unscale"]
    q_d, k_d, v_d, xt_d, x2_d, mb_d, out = (e[k] for k in ("q_d", "k_d", "v_d", "xt_d", "x2_d", "mb_d", "out"))
    QT = N // P
    GROUP = 4
    LEAD = B + 1
    STEPS = DH // B
    SLOTS = STEPS * STAGES
    assert SLOTS == 2 * QT

    pad_ready, q1_in, q2_in, k_in, v_in, xt_in = map(sem, ("pad_ready", "q1_in", "q2_in", "k_in", "v_in", "xt_in"))
    s_ready, max_ready, exp_done = map(sem, ("s_ready", "max_ready", "exp_done"))
    pt1_ready, pt2_ready, pt1_out, pt2_out = map(sem, ("pt1_ready", "pt2_ready", "pt1_out", "pt2_out"))
    av_ready, o_out, ot_ready, o_reduced, o_scaled, inv_ready, x2_ready, x2_saved = map(
        sem, ("av_ready", "o_out", "ot_ready", "o_reduced", "o_scaled", "inv_ready", "x2_ready", "x2_saved"))
    main_done, sum_copied, turned, reduced, q_ready, tanh_ready, high_ready, low_ready = (
        (sem(f"{n}_a"), sem(f"{n}_b")) for n in
        ("main_done", "sum_copied", "turned", "reduced", "q_ready", "tanh_ready", "high_ready", "low_ready"))
    chain, pool_chain, p_ready, pn_ready, const_ready, q_read, q0_ready = map(
        sem, ("chain", "pool_chain", "p_ready", "pn_ready", "const_ready", "q_read", "q0_ready"))
    xn_in, drive_ready, xc_ready, xo_ready, out_turned, out_cp_a, out_cp_v, out_saved = map(
        sem, ("xn_in", "drive_ready", "xc_ready", "xo_ready", "out_turned", "out_cp_act", "out_cp_dve", "out_saved"))

    with ExitStack() as mem:
        sb = lambda name, shape, dt=F32: e["sb"](name, shape, dt, mem)
        qp = sb("qp", [P, 2, N], BF16)
        kp = sb("kp", [P, 2, N], BF16)
        vh = sb("vh", [P, J, DH])
        xt = sb("xt", [P, J, DH])
        x2 = sb("x2", [P, J, DH])
        prob = sb("prob", [P, 2, N])
        prob_t = sb("prob_t", [P, 2, J, BANK])
        nmax = sb("nmax", [P, QT])
        rsum = sb("rsum", [P, QT])
        rinv = sb("rinv", [P, QT])
        o_sb = sb("o_sb", [P, BANK])
        o_red = sb("o_red", [P, GROUP, DH])
        o_nrm = sb("o_nrm", [P, GROUP, DH])
        xn = sb("xn", [P, B, J, DH])
        xc = sb("xc", [P, B, J, DH])
        drive = sb("drive", [P, B, J, DH])
        xo = sb("xo", [P, J, B, DH])
        outs = sb("outs", [P, 2, J, P])
        th16 = sb("th16", [P, 2, 2, J, M_COLS], F16)
        tanh = sb("tanh", [P, J, B])
        sums = sb("sums", [P, 2, 2 * P])
        qs, sq, w3, dmp, ff, ffa, base, isum, kk, acc = (
            sb(n, [P, J, B]) for n in ("qs", "sq", "w3", "dmp", "ff", "ffa", "base", "isum", "kk", "acc"))
        ps_ = [sb(f"p_stage{i}", [P, J, B]) for i in range(2)]
        pm, pr, pt, pn, p0c, racc = (sb(n, [P, J, B]) for n in ("pm", "pr", "pt", "pn", "p0c", "racc"))
        consts = {v: sb(f"const{i}", [P, J, B]) for i, v in enumerate(
            [-BETA] + sorted({c * EPSILON for c in STAGE_C})
            + [0.5 * DT * EPSILON * ALPHA, DT * EPSILON * ALPHA])}

        AC, TP, PT_BANK, O_BANK, S_BANK = (0, 1), (2, 3), 4, 5, 6
        scores_t = bank[:, S_BANK:S_BANK + 2, :]
        F = lambda t: t[:, :, :]
        half_of = lambda t, x: t[:, x * JH:(x + 1) * JH, :]

        def wait(eng, s, value):
            if not isinstance(value, int) or value > 0:
                eng.wait_ge(s, value)

        def run_engine(eng, iteration, begin, output, before=None, attends=True):
            if attends:
                iteration(None, 0, "first")
                with eng.Fori(1, LEAD) as a:
                    iteration(None, a, "full")
            if before:
                before()
            last = NHEAD - 2
            with eng.Fori(0, last) as h:
                begin(h)
                with eng.Fori(0, B) as b:
                    iteration((h, b), h * B + b + LEAD, "full")
                output(h)
            begin(last)
            with eng.Fori(0, B - 2) as b:
                iteration((last, b), b + (last * B + LEAD), "full")
            iteration((last, B - 2), ELEMENTS - 1, "last")
            iteration((last, B - 1), ELEMENTS, "drain")
            output(last)
            begin(NHEAD - 1)
            with eng.Fori(0, B) as b:
                iteration((NHEAD - 1, b), None, None)
            output(NHEAD - 1)

        nothing = lambda h: None

        with nc.Block() as block:
            def load_q(sp, el, half):
                cols = slice(half * BANK, (half + 1) * BANK)
                s = (q1_in, q2_in)[half]
                parts = q_d[el].rearrange("r d t -> (r d) t")
                sp.dma_start(qp[0:3 * DH, 0, cols], parts[:, cols]).then_inc(s, 16)
                sp.dma_start(qp[3 * DH:P, 0, cols], parts[0:DH, cols]).then_inc(s, 16)
                sp.dma_start(qp[0:3 * DH, 1, cols], parts[:, cols]).then_inc(s, 16)

            def load_k(sp, el, b):
                part = lambda i, n: k_d[el, i].unsqueeze(0).broadcast_to([n, DH, N])
                sp.dma_start(kp[0:3 * DH, 0, :], part(0, 3)).then_inc(k_in, 16)
                sp.dma_start(kp[3 * DH:P, 0, :], part(1, 1)).then_inc(k_in, 16)
                sp.dma_start(kp[0:DH, 1, :], part(2, 1)).then_inc(k_in, 16)
                sp.dma_start(kp[DH:3 * DH, 1, :], part(1, 2)).then_inc(k_in, 16)
                sp.dma_start(kp[3 * DH:3 * DH + 3, 1, :], mb_d[b]).then_inc(k_in, 16)

            def sp_iteration(sp, ode, a, mode, b_next=None):
                if a is None:
                    return
                v_dma = lambda: sp.dma_start(vh[:, :, :].rearrange("p j d -> p (j d)"), v_d[a]).then_inc(v_in, 16)
                xt_dma = lambda: sp.dma_start(xt[:, :, :].rearrange("p j d -> p (j d)"), xt_d[a]).then_inc(xt_in, 16)
                more = mode in ("first", "full")
                if mode == "first":
                    v_dma()
                    xt_dma()
                if more:
                    sp.wait_ge(s_ready, a * QT + GROUP)
                    load_q(sp, a + 1, 0)
                if mode != "first":
                    sp.wait_ge(av_ready, a * 2)
                    if mode != "drain":
                        v_dma()
                    sp.wait_ge(x2_ready, a * 2)
                    sp.dma_start(x2_d[a - 1], x2[:, :, :].rearrange("p j d -> p (j d)")).then_inc(x2_saved, 16)
                    if mode != "drain":
                        xt_dma()
                if more:
                    sp.wait_ge(s_ready, a * QT + QT)
                    load_k(sp, a + 1, b_next)
                    load_q(sp, a + 1, 1)

            def sp_load_head(sp, h):
                wait(sp, drive_ready, h)
                wait(sp, xc_ready, h)
                sp.wait_ge(x2_saved, h * (B * 16) + B * 16)
                sp.dma_start(xn[:, :, :, :].rearrange("p b j d -> p b (j d)"),
                             x2_d.rearrange("(h b) p x -> h p b x", b=B)[h]).then_inc(xn_in, 16)

            def sp_store(sp, h):
                for bg in range(2):
                    sp.wait_ge(out_cp_a, FIRST + h * 2 + (bg + 1))
                    sp.wait_ge(out_cp_v, FIRST + h * 2 + (bg + 1))
                    sp.dma_start(out[bg * 4:bg * 4 + 4, bass.ds(h * DH, DH), :],
                                 outs[:, bg, :, :].rearrange("p j i -> p (j i)")).then_inc(out_saved, 16)

            @block.sync
            def _(sp):
                sp.sem_inc(out_saved, FIRST_DMA)
                sp.wait_ge(pad_ready, 4)
                load_q(sp, 0, 0)
                load_k(sp, 0, 0)
                load_q(sp, 0, 1)
                sp_iteration(sp, None, 0, "first", 1)
                with sp.Fori(1, LEAD - 2) as a:
                    sp_iteration(sp, None, a, "full", a + 1)
                sp_iteration(sp, None, LEAD - 2, "full", 0)
                sp_iteration(sp, None, LEAD - 1, "full", 1)
                sp_load_head(sp, 0)

                def head(h):
                    with sp.Fori(0, B - 2) as b:
                        sp_iteration(sp, 1, h * B + b + LEAD, "full", b + 2)
                    sp_iteration(sp, 1, h * B + (B - 2 + LEAD), "full", 0)
                    sp_iteration(sp, 1, h * B + (B - 1 + LEAD), "full", 1)
                    sp_load_head(sp, h + 1)
                    sp_store(sp, h)

                with sp.Fori(0, NHEAD - 2) as h:
                    head(h)
                last = NHEAD - 2
                with sp.Fori(0, B - 2) as b:
                    sp_iteration(sp, 1, b + (last * B + LEAD), "full", b + 2)
                sp_iteration(sp, 1, ELEMENTS - 1, "last")
                sp_iteration(sp, 1, ELEMENTS, "drain")
                sp_load_head(sp, NHEAD - 1)
                sp_store(sp, last)
                sp_store(sp, NHEAD - 1)
                sp.wait_ge(out_saved, FIRST_DMA + NHEAD * 32)

            @block.tensor
            def _(pe):
                pe.wait_ge(pad_ready, 4)

                def scores(a, t):
                    wait(pe, exp_done, a * QT + t)
                    if t == 0:
                        pe.wait_ge(k_in, a * 80 + 80)
                        pe.wait_ge(q1_in, a * 48 + 48)
                    if t == GROUP:
                        pe.wait_ge(q2_in, a * 48 + 48)
                    for half in range(2):
                        for stack in range(2):
                            last = nc.tensor.matmul(bank[:, S_BANK + half, :], qp[:, stack, t * P:(t + 1) * P],
                                                    kp[:, stack, half * BANK:(half + 1) * BANK],
                                                    start=stack == 0, stop=stack == 1)
                    last.then_inc(s_ready, 1)

                def turn(a, t, part):
                    u = a * QT + t
                    if part == 0:
                        pe.wait_ge(exp_done, u + 1)
                        wait(pe, pt2_out, u)
                    else:
                        pe.wait_ge(pt1_out, u + 1)
                    for k in range(4):
                        j = 4 * part + k
                        last = nc.tensor.transpose(bank[:, PT_BANK, k * P:(k + 1) * P],
                                                   prob[:, t % 2, j * P:(j + 1) * P], ident[:, :])
                    last.then_inc((pt1_ready, pt2_ready)[part], 1)

                def values(a, n, piece):
                    gi = a * 2 + n
                    if piece == 0:
                        pe.wait_ge(pt1_out, gi * GROUP + GROUP)
                        pe.wait_ge(pt2_out, gi * GROUP + GROUP)
                        wait(pe, o_reduced, gi)
                        pe.wait_ge(v_in, a * 16 + 16)
                    qh, k = piece // 2, piece % 2
                    cols = slice(qh * BANK // 2, (qh + 1) * BANK // 2)
                    for g in range(G):
                        j = 2 * g + k
                        last = nc.tensor.matmul(bank[g * QUAD:g * QUAD + DH, O_BANK, cols], vh[:, j, :],
                                                prob_t[:, n, j, cols], start=k == 0, stop=k == 1)
                    if piece == 3:
                        last.then_inc(av_ready, 1)

                def turn_values(a, n):
                    gi = a * 2 + n
                    pe.wait_ge(o_out, gi + 1)
                    for k in range(GROUP):
                        last = nc.tensor.transpose(bank[:, O_BANK, k * P:(k + 1) * P], o_sb[:, k * P:(k + 1) * P],
                                                   ident[:, :])
                    last.then_inc(ot_ready, 1)

                def attention(a, mode, k, where):
                    t, odd = k // 2, k % 2
                    prev, cur = mode != "first", mode != "drain"
                    if where == 0:
                        if t < 2 and prev:
                            turn(a - 1, QT - 2 + t, odd)
                        if t >= 2 and cur:
                            turn(a, t - 2, odd)
                    elif odd:
                        if cur:
                            scores(a, t)
                    elif t < 6:
                        if prev:
                            for act_ in {0: ((0, 2), (0, 3)), 1: ((0, "turn"),), 2: ((1, 0),), 3: ((1, 1),),
                                         4: ((1, 2), (1, 3)), 5: ((1, "turn"),)}[t]:
                                if act_[1] == "turn":
                                    turn_values(a - 1, act_[0])
                                else:
                                    values(a - 1, act_[0], act_[1])
                    elif cur:
                        values(a, 0, t - 6)

                def quarter(k, mh, nh, part):
                    for c in range(2):
                        for g in range(G):
                            nq, sel = g // 2, g % 2
                            mj = mh * JH + 2 * sel + c
                            w = cwh[:, part, mj, nh * BANK:(nh + 1) * BANK]\
                                .rearrange("p (c q n) -> p c q n", c=2, q=2)[:, :, nq, :]
                            last = nc.tensor.matmul(
                                bank[g * QUAD:g * QUAD + M_COLS, AC[nh], 0:2 * P], th16[:, k % 2, part, mj, :], w,
                                start=mh == 0 and part == 1 and c == 0, stop=mh == 1 and part == 0 and c == 1,
                                skip_group_check=True)
                    return last

                def turn_sums(K, x):
                    pe.wait_ge(sum_copied[x], K + 1)
                    for c in range(2):
                        last = nc.tensor.transpose(bank[:, TP[x], c * P:(c + 1) * P], sums[:, x, c * P:(c + 1) * P],
                                                   ident[:, :])
                    last.then_inc(turned[x], 1)

                def iteration(ode, a, mode):
                    for k in range(SLOTS):
                        if ode:
                            K = (ode[0] * B + ode[1]) * SLOTS + k
                            pe.wait_ge(high_ready[0], K + 1)
                            quarter(k, 0, 0, 1)
                            pe.wait_ge(low_ready[0], K + 1)
                            quarter(k, 0, 0, 0)
                            quarter(k, 0, 1, 1)
                            pe.wait_ge(high_ready[1], K + 1)
                            quarter(k, 1, 0, 1)
                            pe.wait_ge(low_ready[1], K + 1)
                            quarter(k, 1, 0, 0).then_inc(main_done[0], 1)
                            quarter(k, 0, 1, 0)
                            quarter(k, 1, 1, 1)
                            if k == 0:
                                pe.wait_ge(out_cp_a, FIRST + ode[0] * 2)
                                pe.wait_ge(out_cp_v, FIRST + ode[0] * 2)
                            turn_sums(K, 0)
                            quarter(k, 1, 1, 0).then_inc(main_done[1], 1)
                        if mode:
                            attention(a, mode, k, 0)
                        if ode:
                            turn_sums(K, 1)
                        if mode:
                            attention(a, mode, k, 1)

                def output(h):
                    pe.wait_ge(xo_ready, FIRST + h * DH + DH)
                    for n in range(4):
                        bg, nh = n // 2, n % 2
                        if bg:
                            pe.wait_ge((out_cp_a, out_cp_v)[nh], FIRST + h * 2 + 1)
                        for k in range(JH):
                            last = nc.tensor.transpose(
                                bank[:, TP[nh], k * P:(k + 1) * P],
                                xo[:, nh * JH + k, 4 * bg:4 * bg + 4, :].rearrange("p b d -> p (b d)"), ident[:, :])
                        last.then_inc(out_turned, 1)

                run_engine(pe, iteration, nothing, output)

            @block.scalar
            def _(act):
                def exponent(a, t):
                    u = a * QT + t
                    act.wait_ge(max_ready, u + 1)
                    if not (isinstance(u, int) and u < 2):
                        act.wait_ge(pt2_ready, u - 1)
                    nc.scalar.activation(prob[:, t % 2, :].rearrange("p (c n) -> p c n", c=2), scores_t, ACT.Exp,
                                         bias=nmax[:, t:t + 1], scale=1.0,
                                         accum_out=rsum[:, t:t + 1]).then_inc(exp_done, 1)

                def copy_out(a, t):
                    n, q = t // GROUP, t % GROUP
                    act.wait_ge(pt2_ready, a * QT + t + 1)
                    if q == 0:
                        wait(act, av_ready, (a - 1) * 2 + n + 1)
                    nc.scalar.copy(prob_t[:, n, 4:8, q * P:(q + 1) * P],
                                   bank[:, PT_BANK, :].rearrange("p (k n) -> p k n", n=P)).then_inc(pt2_out, 1)

                def attention(a, mode, k):
                    t, odd = k // 2, k % 2
                    prev, cur = mode != "first", mode != "drain"
                    if odd:
                        if t == 0 and prev:
                            exponent(a - 1, QT - 1)
                        if t >= 1 and cur:
                            exponent(a, t - 1)
                    else:
                        if t < 3 and prev:
                            copy_out(a - 1, QT - 3 + t)
                        if t >= 3 and cur:
                            copy_out(a, t - 3)

                def tanh_high(x, K, parity):
                    act.wait_ge(q_ready[x], K + 1)
                    nc.scalar.activation(half_of(tanh, x), half_of(qs, x), ACT.Tanh).then_inc(tanh_ready[x], 1)
                    act.wait_ge(tanh_ready[x], K + 1)
                    nc.scalar.activation(th16[:, parity, :, x * JH:(x + 1) * JH, H_COL:H_COL + B],
                                         half_of(tanh, x).unsqueeze(1).broadcast_to([P, 2, JH, B]), ACT.Copy,
                                         scale=TANH_SCALE).then_inc(high_ready[x], 1)

                def iteration(ode, a, mode):
                    for k in range(SLOTS):
                        if mode:
                            attention(a, mode, k)
                        if ode:
                            K = (ode[0] * B + ode[1]) * SLOTS + k
                            for x in range(2):
                                act.wait_ge(main_done[x], K + 1)
                                nc.scalar.copy(sums[:, x, :], bank[:, AC[x], 0:2 * P]).then_inc(sum_copied[x], 1)
                            for x in range(2):
                                tanh_high(x, K + 1, (k + 1) % 2)

                def start():
                    act.sem_inc(out_cp_a, FIRST)
                    act.wait_ge(pad_ready, 4)
                    for x in range(2):
                        tanh_high(x, 0, 0)

                def begin(h):
                    act.wait_ge(xn_in, h * 16 + 16)
                    act.wait_ge(xo_ready, FIRST + h * DH)
                    nc.scalar.copy(xc[:, :, :, :], xn[:, :, :, :]).then_inc(xc_ready, 1)

                def output(h):
                    for bg in range(2):
                        act.wait_ge(out_turned, h * 4 + (2 * bg + 1))
                        if bg == 0:
                            act.wait_ge(out_saved, FIRST_DMA + h * 32)
                        nc.scalar.copy(outs[:, bg, 0:JH, :], bank[:, TP[0], :].rearrange("p (j i) -> p j i", i=P))\
                            .then_inc(out_cp_a, 1)

                run_engine(act, iteration, begin, output, before=start)

            @block.gpsimd
            def _(pool):
                for t in (qp, kp):
                    pool.memset(t[:, :, :], 0.0).then_inc(pad_ready, 1)
                pool.wait_ge(pad_ready, 2)
                pool.memset(qp[3 * DH:3 * DH + 3, 1, :], 1.0).then_inc(pad_ready, 1)
                pool.wait_ge(pad_ready, 3)
                pool.memset(th16[:, :, :, :, :], 0.0).then_inc(pad_ready, 1)
                pool.sem_inc(p_ready, FIRST)
                for tile, value in zip(consts.values(), consts):
                    pool.memset(tile[:, :, :], value).then_inc(const_ready, 1)
                pool.wait_ge(const_ready, len(consts))
                count = [0]
                start = [0]

                def link(op, dst, in0, in1):
                    count[0] += 1
                    pool.tensor_tensor(F(dst), F(in0), F(in1), op).then_inc(pool_chain, 1)
                    pool.wait_ge(pool_chain, start[0] + count[0])

                def stage(K, step, s):
                    c = STAGE_C[s]
                    Q = q0 if s == 0 else qs
                    PP = p0 if s == 0 else ps_[(s - 1) % 2]
                    slope = racc if s == 0 else pr
                    if s == 0:
                        pool.wait_ge(p_ready, K + 1)
                    link(ALU.mult, pm, PP, consts[-BETA])
                    if s in (0, 2):
                        link(ALU.add, p0c, p0, consts[c * EPSILON * ALPHA])
                    if s == 0:
                        pool.wait_ge(q0_ready, step + 1)
                    else:
                        for x in range(2):
                            pool.wait_ge(q_ready[x], K + 1)
                    pool.tensor_tensor(F(slope), F(pm), F(Q), ALU.add).then_inc(q_read, 1)
                    pool.wait_ge(q_read, K + 1)
                    if s < STAGES - 1:
                        link(ALU.mult, pt, slope, consts[c * EPSILON])
                        pool.tensor_tensor(F(ps_[s % 2]), F(pt), F(p0c), ALU.add).then_inc(p_ready, 1)
                        pool.wait_ge(p_ready, K + 2)
                        if s > 0:
                            link(ALU.add, racc, racc, pr)
                            link(ALU.add, racc, racc, pr)
                    else:
                        link(ALU.add, racc, racc, pr)
                        link(ALU.mult, pt, racc, consts[c * EPSILON])
                        pool.tensor_tensor(F(pn), F(pt), F(p0c), ALU.add).then_inc(pn_ready, 1)

                def iteration(ode, a, mode):
                    it = ode[0] * B + ode[1]
                    count[0] = 0
                    start[0] = it * POOL_PER_ITERATION
                    for i in range(STEPS):
                        for s in range(STAGES):
                            stage(it * SLOTS + (i * STAGES + s), it * STEPS + i, s)
                    assert count[0] == POOL_PER_ITERATION, count[0]

                run_engine(pool, iteration, nothing, nothing, attends=False)

            @block.vector
            def _(dve):
                count = [0]
                start = [0]

                def made(ins):
                    count[0] += 1
                    ins.then_inc(chain, 1)
                    return start[0] + count[0]

                def row_max(a, t):
                    dve.wait_ge(s_ready, a * QT + t + 1)
                    dve.tensor_reduce(nmax[:, t:t + 1], scores_t, AX.XY, ALU.max, negate=True).then_inc(max_ready, 1)

                def copy_out(a, t):
                    n, q = t // GROUP, t % GROUP
                    dve.wait_ge(pt1_ready, a * QT + t + 1)
                    if q == 0:
                        wait(dve, av_ready, (a - 1) * 2 + n + 1)
                    dve.tensor_copy(prob_t[:, n, 0:4, q * P:(q + 1) * P],
                                    bank[:, PT_BANK, :].rearrange("p (k n) -> p k n", n=P)).then_inc(pt1_out, 1)

                def invert(a, n):
                    dve.wait_ge(exp_done, a * QT + GROUP * (n + 1))
                    g = slice(GROUP * n, GROUP * (n + 1))
                    dve.reciprocal(rinv[:, g], rsum[:, g]).then_inc(inv_ready, 1)

                def copy_values(a, n):
                    dve.wait_ge(av_ready, a * 2 + n + 1)
                    dve.tensor_copy(o_sb[:, :], bank[:, O_BANK, :]).then_inc(o_out, 1)

                def finish(a, n):
                    gi = a * 2 + n
                    g = slice(GROUP * n, GROUP * (n + 1))
                    dve.wait_ge(ot_ready, gi + 1)
                    dve.tensor_reduce(o_red[:, :, :], bank[:, O_BANK, :].rearrange("p (q g d) -> p q d g", q=GROUP, g=G),
                                      AX.X, ALU.add).then_inc(o_reduced, 1)
                    dve.wait_ge(o_reduced, gi + 1)
                    dve.wait_ge(inv_ready, gi + 1)
                    dve.tensor_tensor(o_nrm[:, :, :], o_red[:, :, :],
                                      rinv[:, g].unsqueeze(2).broadcast_to([P, GROUP, DH]), ALU.mult)\
                        .then_inc(o_scaled, 1)
                    dve.wait_ge(o_scaled, gi + 1)
                    dve.wait_ge(xt_in, a * 16 + 16)
                    if n == 0:
                        wait(dve, x2_saved, a * 16)
                    dve.tensor_tensor(x2[:, g, :], xt[:, g, :], o_nrm[:, :, :], ALU.add).then_inc(x2_ready, 1)

                def attention(a, mode, k, where):
                    t, odd = k // 2, k % 2
                    prev, cur = mode != "first", mode != "drain"
                    if where == 1:
                        if odd and prev and t in (0, 4):
                            copy_values(a - 1, t // 4)
                    elif not odd:
                        if t == 0 and prev:
                            row_max(a - 1, QT - 1)
                        if t >= 1 and cur:
                            row_max(a, t - 1)
                        if t == 1 and prev:
                            invert(a - 1, 1)
                        if t == 6 and cur:
                            invert(a, 0)
                    else:
                        if t < 2 and prev:
                            copy_out(a - 1, QT - 2 + t)
                        if t >= 2 and cur:
                            copy_out(a, t - 2)
                        if prev and t in (1, 5):
                            finish(a - 1, t // 4)

                def low_part(x, K, parity):
                    part = th16[:, parity, 0, x * JH:(x + 1) * JH, :]
                    dve.wait_ge(high_ready[x], K + 1)
                    dve.scalar_tensor_tensor(part[:, :, L_COL:L_COL + B], half_of(tanh, x), TANH_SCALE,
                                             part[:, :, H_COL:H_COL + B], ALU.mult, ALU.subtract)\
                        .then_inc(low_ready[x], 1)

                def drive_less_p(K, s, i):
                    dve.wait_ge(p_ready, K + 1)
                    made(dve.tensor_tensor(F(dmp), drive[:, :, :, i].rearrange("p b j -> p j b"),
                                           F(p0 if s == 0 else ps_[(s - 1) % 2]), ALU.subtract))

                def stage(K, k, i, attend):
                    s = k % STAGES
                    c = STAGE_C[s]
                    Q = q0 if s == 0 else qs
                    if s > 0:
                        for x in range(2):
                            dve.wait_ge(q_ready[x], K + 1)
                    n_sq = made(dve.tensor_tensor(F(sq), F(Q), F(Q), ALU.mult))
                    if s > 0:
                        n_kk = made(dve.scalar_tensor_tensor(F(acc if s == 1 else kk), F(isum), unscale[:, 0:1], F(ff),
                                                             ALU.mult, ALU.add))
                    else:
                        drive_less_p(K, s, i)
                    dve.wait_ge(chain, n_sq)
                    n_w3 = made(dve.scalar_tensor_tensor(F(w3), F(sq), -3.0, F(Q), ALU.add, ALU.mult))
                    if s > 1:
                        dve.wait_ge(chain, n_kk)
                        made(dve.scalar_tensor_tensor(F(acc), F(kk), 2.0, F(acc), ALU.mult, ALU.add))
                    dve.wait_ge(chain, n_w3)
                    n_ff = made(dve.scalar_tensor_tensor(F(ff), F(w3), -1.0 / 3.0, F(dmp), ALU.mult, ALU.add))
                    low_part(1, K, k % 2)
                    dve.wait_ge(chain, n_ff)
                    ff_all = ff
                    if s == STAGES - 1:
                        n_all = made(dve.tensor_tensor(F(ffa), F(ff), F(acc), ALU.add))
                        dve.wait_ge(chain, n_all)
                        ff_all = ffa
                    n_base = made(dve.scalar_tensor_tensor(F(base), F(ff_all), c, F(q0), ALU.mult, ALU.add))
                    attend(0)
                    if s < STAGES - 1:
                        drive_less_p(K + 1, s + 1, i)
                    dve.wait_ge(q_read, K + 1)
                    for x in range(2):
                        dve.wait_ge(turned[x], K + 1)
                        dve.tensor_reduce(half_of(isum, x),
                                          sums_view(x), AX.X, ALU.add).then_inc(reduced[x], 1)
                        dve.wait_ge(reduced[x], K + 1)
                        if x == 0:
                            dve.wait_ge(chain, n_base)
                        dve.scalar_tensor_tensor(half_of(qs, x), half_of(isum, x), isum_c[:, s:s + 1],
                                                 half_of(base, x), ALU.mult, ALU.add).then_inc(q_ready[x], 1)
                        if x == 0:
                            attend(1)
                            low_part(0, K + 1, (k + 1) % 2)

                def sums_view(x):
                    return bank[:, TP[x], 0:2 * P].rearrange("p (k m b) -> p k b m", k=4, m=4)[:, :, 0:B, :]

                def iteration(ode, a, mode):
                    if ode:
                        h, b = ode
                        it = h * B + b
                        count[0] = 0
                        start[0] = it * CHAIN_PER_ITERATION
                    for k in range(SLOTS):
                        attend = lambda where: attention(a, mode, k, where) if mode else None
                        if not ode:
                            attend(0)
                            attend(1)
                        else:
                            K = it * SLOTS + k
                            s = k % STAGES
                            i = b * STEPS + k // STAGES
                            if k == 0:
                                dve.wait_ge(drive_ready, h + 1)
                            if s == 0:
                                dve.wait_ge(q0_ready, it * STEPS + k // STAGES + 1)
                            stage(K, k, i, attend)
                            if s == STAGES - 1:
                                for x in range(2):
                                    dve.wait_ge(q_ready[x], K + 2)
                                dve.tensor_scalar(F(q0), F(qs), -CLAMP, CLAMP, ALU.max, ALU.min).then_inc(q0_ready, 1)
                                dve.wait_ge(pn_ready, it * STEPS + k // STAGES + 1)
                                dve.tensor_scalar(F(p0), F(pn), -CLAMP, CLAMP, ALU.max, ALU.min).then_inc(p_ready, 1)
                                dve.wait_ge(q0_ready, it * STEPS + k // STAGES + 2)
                                if k == STAGES - 1:
                                    dve.wait_ge(xc_ready, h + 1)
                                dve.tensor_tensor(xo[:, :, :, i], xc[:, :, :, i].rearrange("p b j -> p j b"), F(q0),
                                                  ALU.add).then_inc(xo_ready, 1)
                    if ode:
                        assert count[0] == CHAIN_PER_ITERATION, count[0]

                def start_ode():
                    dve.sem_inc(q0_ready, FIRST)
                    dve.sem_inc(xo_ready, FIRST)
                    dve.sem_inc(out_cp_v, FIRST)
                    for x in range(2):
                        dve.tensor_copy(half_of(qs, x), half_of(q0, x)).then_inc(q_ready[x], 1)
                    dve.wait_ge(pad_ready, 4)
                    low_part(0, 0, 0)

                def begin(h):
                    dve.wait_ge(xn_in, h * 16 + 16)
                    dve.tensor_tensor(drive[:, :, :, :], xn[:, :, :, :],
                                      bias_col[:, :].unsqueeze(1).unsqueeze(3).broadcast_to([P, B, J, DH]),
                                      ALU.add).then_inc(drive_ready, 1)

                def output(h):
                    for bg in range(2):
                        dve.wait_ge(out_turned, h * 4 + (2 * bg + 2))
                        if bg == 0:
                            dve.wait_ge(out_saved, FIRST_DMA + h * 32)
                        dve.tensor_copy(outs[:, bg, JH:J, :], bank[:, TP[1], :].rearrange("p (j i) -> p j i", i=P))\
                            .then_inc(out_cp_v, 1)

                run_engine(dve, iteration, begin, output, before=start_ode)


POOL_PER_ITERATION = 4 * (3 + 4 + 5 + 3)
CHAIN_PER_ITERATION = 4 * (5 + 6 + 7 + 8)


_INS = ["x", "cond_2048", "L0_cond_Wq", "L0_cond_Wk", "L0_cond_Wv", "L0_cond_b", "L1_cond_coupling", "L1_cond_bias"]
_OUTS = [((8, 512, 1024), "float32")]


def kernel(**inputs):
    import numpy as _np
    import concourse.bacc as _bacc
    from concourse import mybir as _mybir
    from concourse.bass_utils import run_bass_kernel_spmd as _run

    nc = _bacc.Bacc("TRN2", target_bir_lowering=False, num_devices=1)
    arrays, args = {}, []
    for name in _INS:
        a = _np.ascontiguousarray(inputs[name])
        arrays[f"in_{name}_dram"] = a
        args.append(nc.dram_tensor(f"in_{name}_dram", a.shape, _mybir.dt.from_np(a.dtype), kind="ExternalInput").ap())
    for i, (shape, dtype) in enumerate(_OUTS):
        dt = _mybir.dt.from_np(_np.dtype(dtype))
        args.append(nc.dram_tensor(f"out_{i}_dram", shape, dt, kind="ExternalOutput").ap())
    build_program(nc, *args)
    r = _run(nc, [arrays], core_ids=[0])
    return r.results[0]["out_0_dram"]
```

```python
from contextlib import ExitStack

import concourse.bass as bass
from concourse import mybir

F32 = mybir.dt.float32
F16 = mybir.dt.float16
BF16 = mybir.dt.bfloat16
I32 = mybir.dt.int32
ALU = mybir.AluOpType
ACT = mybir.ActivationFunctionType
AX = mybir.AxisListType
ALL_MAX = bass.bass_isa.ReduceOp.max

P = 128
QUAD = 32
BANK = 512
NHEAD = 16
NEG_INF = -1e30

FIRST, FIRST_DMA = 1, 16

DT, EPSILON, ALPHA, BETA, CLAMP = 0.01, 0.08, 0.7, 0.8, 20.0
STAGES = 4
STAGE_C = (0.5 * DT, 0.5 * DT, DT, DT / 6.0)

W_EXP = 14
LOW_SCALE = 2.0 ** 11
H_COL, L_COL, M_COLS = 0, 16, 24


def build_program(nc, x, cond, Wq, Wk, Wv, att_b, coupling, ode_bias, out):
    B, C, N = x.shape
    DH = C // NHEAD
    CC = C // P
    J = N // P
    G = P // QUAD
    JH = J // 2
    ELEMENTS = NHEAD * B
    SCALE = float(DH) ** -0.5

    q_d = nc.dram_tensor("q_scratch", [ELEMENTS, 3, DH, N], BF16).ap()
    k_d = nc.dram_tensor("k_scratch", [ELEMENTS, 3, DH, N], BF16).ap()
    v_d = nc.dram_tensor("v_scratch", [ELEMENTS, P, J * DH], F32).ap()
    xt_d = nc.dram_tensor("xt_scratch", [ELEMENTS, P, J * DH], F32).ap()
    x2_d = nc.dram_tensor("x2_scratch", [ELEMENTS, P, J * DH], F32).ap()
    mb_d = nc.dram_tensor("mask_bias_scratch", [B, 3, N], BF16).ap()

    with ExitStack() as ctx:
        def sb(name, shape, dt=F32, where=ctx):
            return where.enter_context(nc.sbuf_tensor(name, shape, dt))

        def sem(name):
            return ctx.enter_context(nc.semaphore(name))

        bank = ctx.enter_context(nc.psum_tensor("bank", [P, 8, BANK], F32))
        ident = sb("ident", [P, P])
        cwh = sb("cwh", [P, 2, J, N], F16)
        isum_c = sb("isum_c", [P, STAGES])
        unscale = sb("unscale", [P, 1])
        bias_col = sb("bias_col", [P, J])
        q0 = sb("q0", [P, J, B])
        p0 = sb("p0", [P, J, B])

        setup(nc, locals())
        project(nc, locals())
        attend_and_scan(nc, locals())


def setup(nc, e):
    cond, coupling, ode_bias, att_b = e["cond"], e["coupling"], e["ode_bias"], e["att_b"]
    B, N, J = e["B"], e["N"], e["J"]
    ident, cwh, bias_col, q0, p0, bank = e["ident"], e["cwh"], e["bias_col"], e["q0"], e["p0"], e["bank"]
    isum_c, unscale = e["isum_c"], e["unscale"]
    sem = e["sem"]
    id_step, coup_in, small_in, mb_step, mb_out = map(sem, ("id_step", "coup_in", "small_in", "mb_step", "mb_out"))
    scale_step, row_max, all_max = map(sem, ("scale_step", "row_max", "all_max"))
    group_ready, state_out, high_out, low_out = map(sem, ("setup_group_ready", "state_out", "high_out", "low_out"))
    NG = J * J // 4

    with ExitStack() as mem:
        coup = e["sb"]("coup", [P, J, N], F32, mem)
        cond_sb = e["sb"]("cond_sb", [B, N], F32, mem)
        bias_row = e["sb"]("bias_row", [J, P], F32, mem)
        mask_bias = e["sb"]("mask_bias", [B, N], F32, mem)
        mask_rest = e["sb"]("mask_rest", [B, N], F32, mem)
        mask_parts = e["sb"]("mask_parts", [B, 3, N], BF16, mem)
        inv = e["sb"]("inv", [B, N], F32, mem)
        b_col = e["sb"]("b_col", [B, 1], F32, mem)
        part_max = e["sb"]("part_max", [P, 1], F32, mem)
        abs_max = e["sb"]("abs_max", [P, 1], F32, mem)
        abs_floor = e["sb"]("abs_floor", [P, 1], F32, mem)
        exponent = e["sb"]("exponent", [P, 1], I32, mem)
        w_scale = e["sb"]("w_scale", [P, 1], I32, mem)

        with nc.Block() as block:
            @block.sync
            def _(sp):
                sp.dma_start(coup[:, :, :], coupling.rearrange("(j p) m -> p j m", p=P)).then_inc(coup_in, 16)
                sp.dma_start(cond_sb[:, :], cond).then_inc(small_in, 16)
                sp.dma_start(bias_row[:, :], ode_bias.rearrange("(j p) -> j p", p=P)).then_inc(small_in, 16)
                sp.dma_start(b_col[:, :], att_b.rearrange("(a n) -> a n", a=1).broadcast_to([B, 1]))\
                    .then_inc(small_in, 16)
                sp.wait_ge(mb_step, 7)
                sp.dma_start(e["mb_d"], mask_parts[:, :, :]).then_inc(mb_out, 16)
                sp.wait_ge(mb_out, 16)

            @block.gpsimd
            def _(pool):
                nc.gpsimd.memset(ident[:, :], 0.0).then_inc(id_step, 1)
                pool.wait_ge(id_step, 1)
                nc.gpsimd.affine_select(out=ident[:, :], in_=ident[:, :], compare_op=ALU.not_equal, fill=1.0,
                                        base=0, pattern=[[-1, P]], channel_multiplier=1).then_inc(id_step, 1)
                pool.wait_ge(row_max, 1)
                nc.gpsimd.partition_all_reduce(abs_max[:, :], part_max[:, :], P, ALL_MAX).then_inc(all_max, 1)

            @block.tensor
            def _(pe):
                pe.wait_ge(id_step, 2)
                pe.wait_ge(small_in, 48)
                for j in range(J):
                    nc.tensor.transpose(bank[:, 0, j * B:(j + 1) * B], cond_sb[:, j * P:(j + 1) * P],
                                        ident[0:B, 0:B])
                nc.tensor.transpose(bank[:, 0, J * B:J * B + J], bias_row[:, :],
                                    ident[0:J, 0:J]).then_inc(group_ready, 1)
                pe.wait_ge(coup_in, 16)
                for g in range(NG):
                    if g == 7:
                        pe.wait_ge(state_out, 1)
                    if g > 7:
                        pe.wait_ge(low_out, g - 7)
                    for k in range(4):
                        mj, nj = g // 2, 4 * (g % 2) + k
                        last = nc.tensor.transpose(bank[:, (g + 1) % 8, k * P:(k + 1) * P],
                                                   coup[:, nj, mj * P:(mj + 1) * P], ident[:, :])
                    last.then_inc(group_ready, 1)

            def w_half(part, g):
                return cwh[:, part, g // 2, g % 2 * BANK:(g % 2 + 1) * BANK]

            @block.vector
            def _(dve):
                dve.wait_ge(small_in, 48)
                dve.tensor_scalar(inv[:, :], cond_sb[:, :], -1.0, 1.0, ALU.mult, ALU.add).then_inc(mb_step, 1)
                dve.wait_ge(mb_step, 1)
                dve.tensor_scalar(inv[:, :], inv[:, :], NEG_INF, None, ALU.mult).then_inc(mb_step, 1)
                dve.wait_ge(mb_step, 2)
                dve.scalar_tensor_tensor(mask_bias[:, :], cond_sb[:, :], b_col[:, 0:1], inv[:, :],
                                         ALU.mult, ALU.add).then_inc(mb_step, 1)
                dve.wait_ge(mb_step, 3)
                dve.tensor_copy(mask_parts[:, 0, :], mask_bias[:, :]).then_inc(mb_step, 1)
                dve.wait_ge(mb_step, 4)
                dve.tensor_tensor(mask_rest[:, :], mask_bias[:, :], mask_parts[:, 0, :], ALU.subtract)\
                    .then_inc(mb_step, 1)
                dve.wait_ge(mb_step, 5)
                dve.tensor_copy(mask_parts[:, 1, :], mask_rest[:, :]).then_inc(mb_step, 1)
                dve.wait_ge(mb_step, 6)
                dve.tensor_tensor(mask_parts[:, 2, :], mask_rest[:, :], mask_parts[:, 1, :], ALU.subtract)\
                    .then_inc(mb_step, 1)

                dve.wait_ge(coup_in, 16)
                dve.tensor_reduce(part_max[:, :], coup[:, :, :], AX.XY, ALU.max, apply_absolute_value=True)\
                    .then_inc(row_max, 1)
                dve.wait_ge(all_max, 1)
                dve.tensor_scalar(abs_floor[:, :], abs_max[:, :], 2.0 ** -100, None, ALU.max).then_inc(scale_step, 1)
                dve.wait_ge(scale_step, 1)
                dve.tensor_scalar(exponent[:, :], abs_floor[:, :].bitcast(I32), 0x7f800000, None, ALU.bitwise_and)\
                    .then_inc(scale_step, 1)
                dve.wait_ge(scale_step, 2)
                dve.tensor_scalar(w_scale[:, :], exponent[:, :], -1.0, float((254 + W_EXP) << 23), ALU.mult, ALU.add)\
                    .then_inc(scale_step, 1)
                undo = 2.0 ** -W_EXP
                for s, c in enumerate(STAGE_C):
                    dve.tensor_scalar(isum_c[:, s:s + 1], exponent[:, :].bitcast(F32), c * undo, None, ALU.mult)
                dve.tensor_scalar(unscale[:, :], exponent[:, :].bitcast(F32), undo, None, ALU.mult)

                dve.wait_ge(group_ready, 1)
                state = bank[:, 0, 0:J * B].rearrange("p (j b) -> p j b", b=B)
                dve.tensor_copy(q0[:, :, :], state)
                dve.tensor_copy(p0[:, :, :], state)
                dve.tensor_copy(bias_col[:, :], bank[:, 0, J * B:J * B + J]).then_inc(state_out, 1)
                dve.wait_ge(scale_step, 3)
                for g in range(NG):
                    dve.wait_ge(high_out, g + 1)
                    dve.scalar_tensor_tensor(w_half(1, g), bank[:, (g + 1) % 8, :], w_scale[:, :].bitcast(F32),
                                             w_half(0, g), ALU.mult, ALU.subtract).then_inc(low_out, 1)

            @block.scalar
            def _(act):
                act.wait_ge(scale_step, 3)
                for g in range(NG):
                    act.wait_ge(group_ready, g + 2)
                    nc.scalar.activation(w_half(0, g), bank[:, (g + 1) % 8, :], ACT.Copy,
                                         scale=w_scale[:, :].bitcast(F32)).then_inc(high_out, 1)


def project(nc, e):
    x, cond, B, C, N, CC, J, DH, SCALE = (e[k] for k in ("x", "cond", "B", "C", "N", "CC", "J", "DH", "SCALE"))
    ident, bank, sem = e["ident"], e["bank"], e["sem"]
    q_d, k_d, v_d, xt_d = e["q_d"], e["k_d"], e["v_d"], e["xt_d"]
    w_in, w_group, w_out = map(sem, ("w_in", "w_group", "w_out"))
    x_in = [sem("x_in0"), sem("x_in1")]
    unit_ready, unit_out_a, unit_out_v = map(sem, ("unit_ready", "unit_out_act", "unit_out_dve"))
    q_saved = [sem("q_saved0"), sem("q_saved1")]
    k_saved = [sem("k_saved0"), sem("k_saved1")]
    part0_ready, rest_ready, part1_ready, part2_ready = map(
        sem, ("part0_ready", "rest_ready", "part1_ready", "part2_ready"))
    v_saved, xt_saved = sem("v_saved"), sem("xt_saved")
    units = [(kind, oc, half) for oc in range(CC) for kind in "qk" for half in range(2)]
    units += [("v", j, 0) for j in range(J)] + [("x", j, 0) for j in range(J)]
    NU = len(units)
    NA = sum(k in "qv" for k, _, _ in units)
    ND = NU - NA
    NQK = sum(k in "qk" for k, _, _ in units)
    assert NU % 8 == 0
    a_before = [sum(k in "qv" for k, _, _ in units[:n]) for n in range(NU + 1)]

    with ExitStack() as mem:
        sb = lambda name, shape: e["sb"](name, shape, F32, mem)
        w_nat = sb("w_nat", [P, 3, CC, C])
        w_t = sb("w_t", [P, 3, CC, C])
        xs = sb("xs", [P, 2, CC, N])
        mask_bc = sb("mask_bc", [P, 2, N])
        st = {k: e["sb"](f"{k}_st", [P, 2, 3, N], BF16, mem) for k in "qk"}
        full = sb("full", [P, 2, BANK])
        rest = sb("rest", [P, 2, BANK])
        v_st = sb("v_st", [P, NHEAD, J, DH])
        xt_st = sb("xt_st", [P, NHEAD, J, DH])

        with nc.Block() as block:
            def load_x(sp, par, b):
                sp.dma_start(xs[:, par, :, :], x[b].rearrange("(c p) t -> p c t", p=P)).then_inc(x_in[par], 16)
                sp.dma_start(mask_bc[:, par, :], cond[b].rearrange("(a t) -> a t", a=1).broadcast_to([P, N]))\
                    .then_inc(x_in[par], 16)

            def save_batch(sp, b):
                for oc in range(CC):
                    for i, (dst, saved) in enumerate(((q_d, q_saved), (k_d, k_saved))):
                        sp.wait_ge(part2_ready, b * NQK + (4 * oc + 2 * i + 2))
                        for part in range(3):
                            sp.dma_start(dst.rearrange("(h b) r d t -> h b r d t", b=B)[4 * oc:4 * oc + 4, b, part, :, :],
                                         st["qk"[i]][:, oc % 2, part, :]).then_inc(saved[oc % 2], 16)
                sp.wait_ge(unit_out_a, FIRST + b * NA + NA)
                sp.dma_start(v_d.rearrange("(h b) p x -> b p h x", b=B)[b],
                             v_st[:, :, :, :].rearrange("p h j d -> p h (j d)")).then_inc(v_saved, 16)
                sp.wait_ge(unit_out_v, FIRST + b * ND + ND)
                sp.dma_start(xt_d.rearrange("(h b) p x -> b p h x", b=B)[b],
                             xt_st[:, :, :, :].rearrange("p h j d -> p h (j d)")).then_inc(xt_saved, 16)

            @block.sync
            def _(sp):
                for i, w in enumerate((e["Wq"], e["Wk"], e["Wv"])):
                    sp.dma_start(w_nat[:, i, :, :], w.rearrange("(j p) c -> p j c", p=P)).then_inc(w_in, 16)
                load_x(sp, 0, 0)
                for s in q_saved + k_saved + [v_saved, xt_saved]:
                    sp.sem_inc(s, FIRST_DMA)

                def pair(bp, last):
                    load_x(sp, 1, bp * 2 + 1)
                    save_batch(sp, bp * 2)
                    if not last:
                        load_x(sp, 0, bp * 2 + 2)
                    save_batch(sp, bp * 2 + 1)

                with sp.Fori(0, B // 2 - 1) as bp:
                    pair(bp, False)
                pair(B // 2 - 1, True)
                for s in q_saved + k_saved:
                    sp.wait_ge(s, FIRST_DMA + 48 * B * CC // 2)
                sp.wait_ge(v_saved, FIRST_DMA + 16 * B)
                sp.wait_ge(xt_saved, FIRST_DMA + 16 * B)

            @block.tensor
            def _(pe):
                pe.wait_ge(w_in, 48)
                for i in range(3):
                    for cj in range(CC):
                        g = i * CC + cj
                        if g >= 8:
                            pe.wait_ge(w_out, g - 8 + 1)
                        for oj in range(CC):
                            last = nc.tensor.transpose(bank[:, g % 8, oj * P:(oj + 1) * P],
                                                       w_nat[:, i, oj, cj * P:(cj + 1) * P], ident[:, :])
                        last.then_inc(w_group, 1)
                pe.wait_ge(w_out, 3 * CC)
                with pe.Fori(0, B // 2) as bp:
                    for par in range(2):
                        b = bp * 2 + par
                        pe.wait_ge(x_in[par], bp * 32 + 32)
                        for n, (kind, a, half) in enumerate(units):
                            if n >= 8:
                                old = n - 7
                                pe.wait_ge(unit_out_a, FIRST + b * NA + a_before[old])
                                pe.wait_ge(unit_out_v, FIRST + b * ND + (old - a_before[old]))
                            elif n == 0:
                                pe.wait_ge(unit_out_a, FIRST + b * NA)
                                pe.wait_ge(unit_out_v, FIRST + b * ND)
                            dst = bank[:, n % 8, :]
                            if kind in "qk":
                                for cj in range(CC):
                                    last = nc.tensor.matmul(
                                        dst, w_t[:, "qk".index(kind), cj, a * P:(a + 1) * P],
                                        xs[:, par, cj, half * BANK:(half + 1) * BANK],
                                        start=cj == 0, stop=cj == CC - 1)
                            elif kind == "v":
                                for cj in range(CC):
                                    last = nc.tensor.matmul(dst, xs[:, par, cj, a * P:(a + 1) * P], w_t[:, 2, cj, :],
                                                            start=cj == 0, stop=cj == CC - 1)
                            else:
                                for cj in range(CC):
                                    last = nc.tensor.transpose(dst[:, cj * P:(cj + 1) * P],
                                                               xs[:, par, cj, a * P:(a + 1) * P], ident[:, :])
                            last.then_inc(unit_ready, 1)

            def split_unit(eng, g, kind, a, half, n, which):
                parity = n % 2
                cols = slice(half * BANK, (half + 1) * BANK)
                parts = st[kind][:, a % 2, :, cols]
                if which == "act":
                    nc.scalar.copy(parts[:, 0, :], full[:, parity, :]).then_inc(part0_ready, 1)
                    eng.wait_ge(rest_ready, g + 1)
                    nc.scalar.copy(parts[:, 1, :], rest[:, parity, :]).then_inc(part1_ready, 1)
                else:
                    eng.wait_ge(part0_ready, g + 1)
                    nc.vector.tensor_tensor(rest[:, parity, :], full[:, parity, :], parts[:, 0, :], ALU.subtract)\
                        .then_inc(rest_ready, 1)
                    eng.wait_ge(part1_ready, g + 1)
                    nc.vector.tensor_tensor(parts[:, 2, :], rest[:, parity, :], parts[:, 1, :], ALU.subtract)\
                        .then_inc(part2_ready, 1)

            @block.scalar
            def _(act):
                act.sem_inc(unit_out_a, FIRST)
                with act.Fori(0, B // 2) as bp:
                    for par in range(2):
                        b = bp * 2 + par
                        for n, (kind, a, half) in enumerate(units):
                            if kind == "x":
                                continue
                            if kind == "v":
                                if a == 0:
                                    act.wait_ge(v_saved, FIRST_DMA + b * 16)
                                act.wait_ge(unit_ready, b * NU + (n + 1))
                                nc.scalar.copy(v_st[:, :, a, :], bank[:, n % 8, :].rearrange("p (h d) -> p h d", d=DH))\
                                    .then_inc(unit_out_a, 1)
                                continue
                            if kind == "q":
                                act.wait_ge(unit_ready, b * NU + (n + 1))
                                nc.scalar.activation(full[:, n % 2, :], bank[:, n % 8, :], ACT.Copy, scale=SCALE)\
                                    .then_inc(unit_out_a, 1)
                            if half == 0:
                                saved = (q_saved if kind == "q" else k_saved)[a % 2]
                                act.wait_ge(saved, FIRST_DMA + b * 96 + 48 * (a // 2))
                            if kind == "q":
                                act.wait_ge(unit_out_a, FIRST + b * NA + a_before[n + 1])
                            else:
                                act.wait_ge(unit_out_v, FIRST + b * ND + (n + 1 - a_before[n + 1]))
                            split_unit(act, b * NQK + n, kind, a, half, n, "act")

            @block.vector
            def _(dve):
                for g in range(3 * CC):
                    dve.wait_ge(w_group, g + 1)
                    dve.tensor_copy(w_t[:, g // CC, g % CC, :], bank[:, g % 8, :]).then_inc(w_out, 1)
                dve.sem_inc(unit_out_v, FIRST)
                with dve.Fori(0, B // 2) as bp:
                    for par in range(2):
                        b = bp * 2 + par
                        for n, (kind, a, half) in enumerate(units):
                            if kind == "v":
                                continue
                            if kind == "x":
                                if a == 0:
                                    dve.wait_ge(xt_saved, FIRST_DMA + b * 16)
                                dve.wait_ge(unit_ready, b * NU + (n + 1))
                                dve.tensor_copy(xt_st[:, :, a, :], bank[:, n % 8, :].rearrange("p (h d) -> p h d", d=DH))\
                                    .then_inc(unit_out_v, 1)
                                continue
                            if kind == "k":
                                if n == 2:
                                    dve.wait_ge(x_in[par], bp * 32 + 32)
                                dve.wait_ge(unit_ready, b * NU + (n + 1))
                                dve.tensor_tensor(full[:, n % 2, :], bank[:, n % 8, :],
                                                  mask_bc[:, par, half * BANK:(half + 1) * BANK], ALU.mult)\
                                    .then_inc(unit_out_v, 1)
                            split_unit(dve, b * NQK + n, kind, a, half, n, "dve")


def attend_and_scan(nc, e):
    B, N, J, DH, G, JH, ELEMENTS = (e[k] for k in ("B", "N", "J", "DH", "G", "JH", "ELEMENTS"))
    ident, bank, cwh, bias_col, q0, p0, sem = (e[k] for k in ("ident", "bank", "cwh", "bias_col", "q0", "p0", "sem"))
    isum_c, unscale = e["isum_c"], e["unscale"]
    q_d, k_d, v_d, xt_d, x2_d, mb_d, out = (e[k] for k in ("q_d", "k_d", "v_d", "xt_d", "x2_d", "mb_d", "out"))
    QT = N // P
    GROUP = 4
    LEAD = B + 1
    STEPS = DH // B
    SLOTS = STEPS * STAGES
    assert SLOTS == 2 * QT

    pad_ready, q1_in, q2_in, k_in, v_in, xt_in = map(sem, ("pad_ready", "q1_in", "q2_in", "k_in", "v_in", "xt_in"))
    s_ready, max_ready, exp_done = map(sem, ("s_ready", "max_ready", "exp_done"))
    pt1_ready, pt2_ready, pt1_out, pt2_out = map(sem, ("pt1_ready", "pt2_ready", "pt1_out", "pt2_out"))
    av_ready, o_out, ot_ready, o_reduced, o_scaled, inv_ready, x2_ready, x2_saved = map(
        sem, ("av_ready", "o_out", "ot_ready", "o_reduced", "o_scaled", "inv_ready", "x2_ready", "x2_saved"))
    q_ready, tanh_ready, high_ready, low_ready = (
        (sem(f"{n}_a"), sem(f"{n}_b")) for n in ("q_ready", "tanh_ready", "high_ready", "low_ready"))
    main_done, sums_turned, isum_ready, sq_ready, dmp_ready = map(sem, (
        "main_done", "sums_turned", "isum_ready", "sq_ready", "dmp_ready"))
    chain, pool_chain, p_ready, pn_ready, const_ready, q_read, q0_ready = map(
        sem, ("chain", "pool_chain", "p_ready", "pn_ready", "const_ready", "q_read", "q0_ready"))
    xn_in, drive_ready, xc_ready, xo_ready, out_turned, out_cp_a, out_cp_v, out_saved = map(
        sem, ("xn_in", "drive_ready", "xc_ready", "xo_ready", "out_turned", "out_cp_act", "out_cp_dve", "out_saved"))

    with ExitStack() as mem:
        sb = lambda name, shape, dt=F32: e["sb"](name, shape, dt, mem)
        qp = sb("qp", [P, 2, N], BF16)
        kp = sb("kp", [P, 2, N], BF16)
        vh = sb("vh", [P, J, DH])
        xt = sb("xt", [P, J, DH])
        x2 = sb("x2", [P, J, DH])
        prob = sb("prob", [P, 2, N])
        prob_t = sb("prob_t", [P, 2, J, BANK])
        nmax = sb("nmax", [P, QT])
        rsum = sb("rsum", [P, QT])
        rinv = sb("rinv", [P, QT])
        o_sb = sb("o_sb", [P, BANK])
        o_red = sb("o_red", [P, GROUP, DH])
        o_nrm = sb("o_nrm", [P, GROUP, DH])
        xn = sb("xn", [P, B, J, DH])
        xc = sb("xc", [P, B, J, DH])
        drive = sb("drive", [P, B, J, DH])
        xo = sb("xo", [P, J, B, DH])
        outs = sb("outs", [P, 2, J, P])
        th16 = sb("th16", [P, 2, J, M_COLS], F16)
        tanh = sb("tanh", [P, J, B])
        high = sb("high", [P, J, B])
        sums = sb("sums", [P, J, QUAD])
        dmp = [sb(f"dmp{i}", [P, J, B]) for i in range(2)]
        qs, sq, w3, ff, ffa, base, isum, kk, acc = (
            sb(n, [P, J, B]) for n in ("qs", "sq", "w3", "ff", "ffa", "base", "isum", "kk", "acc"))
        ps_ = [sb(f"p_stage{i}", [P, J, B]) for i in range(2)]
        pm, pr, pt, pn, p0c, racc = (sb(n, [P, J, B]) for n in ("pm", "pr", "pt", "pn", "p0c", "racc"))
        consts = {v: sb(f"const{i}", [P, J, B]) for i, v in enumerate(
            [-BETA] + sorted({c * EPSILON for c in STAGE_C})
            + [0.5 * DT * EPSILON * ALPHA, DT * EPSILON * ALPHA])}

        MAIN_BANK, OUT_BANKS, PT_BANK, O_BANK, S_BANK = 0, (1, 2, 3, 2), 4, 5, 6

        def scores_bank(t, alone):
            return 2 if alone and t % 2 == 0 else S_BANK

        F = lambda t: t[:, :, :]
        half_of = lambda t, x: t[:, x * JH:(x + 1) * JH, :]

        def wait(eng, s, value):
            if not isinstance(value, int) or value > 0:
                eng.wait_ge(s, value)

        def run_engine(eng, iteration, begin, output, before=None, attends=True, begin_first=False, unroll=1):
            def between(h):
                for part, head in ((begin, h + 1), (output, h)) if begin_first else ((output, h), (begin, h + 1)):
                    part(head)

            if attends:
                iteration(None, 0, "first")
                with eng.Fori(1, LEAD) as a:
                    iteration(None, a, "full")
            if before:
                before()
            last = NHEAD - 2
            begin(0)
            with eng.Fori(0, last) as h:
                with eng.Fori(0, B // unroll) as bu:
                    for u in range(unroll):
                        b = bu * unroll + u
                        iteration((h, b), h * B + b + LEAD, "full")
                between(h)
            with eng.Fori(0, (B - 2) // unroll) as bu:
                for u in range(unroll):
                    b = bu * unroll + u
                    iteration((last, b), b + (last * B + LEAD), "full")
            iteration((last, B - 2), ELEMENTS - 1, "last")
            iteration((last, B - 1), ELEMENTS, "drain")
            between(last)
            with eng.Fori(0, B) as b:
                iteration((NHEAD - 1, b), None, None)
            output(NHEAD - 1)

        nothing = lambda h: None

        with nc.Block() as block:
            def load_q(sp, el, half):
                cols = slice(half * BANK, (half + 1) * BANK)
                s = (q1_in, q2_in)[half]
                parts = q_d[el].rearrange("r d t -> (r d) t")
                sp.dma_start(qp[0:3 * DH, 0, cols], parts[:, cols]).then_inc(s, 16)
                sp.dma_start(qp[3 * DH:P, 0, cols], parts[0:DH, cols]).then_inc(s, 16)
                sp.dma_start(qp[0:3 * DH, 1, cols], parts[:, cols]).then_inc(s, 16)

            def load_k(sp, el, b):
                part = lambda i, n: k_d[el, i].unsqueeze(0).broadcast_to([n, DH, N])
                sp.dma_start(kp[0:3 * DH, 0, :], part(0, 3)).then_inc(k_in, 16)
                sp.dma_start(kp[3 * DH:P, 0, :], part(1, 1)).then_inc(k_in, 16)
                sp.dma_start(kp[0:DH, 1, :], part(2, 1)).then_inc(k_in, 16)
                sp.dma_start(kp[DH:3 * DH, 1, :], part(1, 2)).then_inc(k_in, 16)
                sp.dma_start(kp[3 * DH:3 * DH + 3, 1, :], mb_d[b]).then_inc(k_in, 16)

            def sp_iteration(sp, ode, a, mode, b_next=None, next_head=None):
                if a is None:
                    return
                v_dma = lambda: sp.dma_start(vh[:, :, :].rearrange("p j d -> p (j d)"), v_d[a]).then_inc(v_in, 16)
                xt_dma = lambda: sp.dma_start(xt[:, :, :].rearrange("p j d -> p (j d)"), xt_d[a]).then_inc(xt_in, 16)
                more = mode in ("first", "full")
                if mode == "first":
                    v_dma()
                    xt_dma()
                if more:
                    sp.wait_ge(s_ready, a * QT + GROUP)
                    load_q(sp, a + 1, 0)
                if mode != "first":
                    sp.wait_ge(av_ready, a * 2)
                    if mode != "drain":
                        v_dma()
                    sp.wait_ge(x2_ready, a * 2)
                    sp.dma_start(x2_d[a - 1], x2[:, :, :].rearrange("p j d -> p (j d)")).then_inc(x2_saved, 16)
                    if mode != "drain":
                        xt_dma()
                if next_head is not None:
                    sp_load_head(sp, next_head)
                if more:
                    sp.wait_ge(s_ready, a * QT + QT)
                    load_k(sp, a + 1, b_next)
                    load_q(sp, a + 1, 1)

            def sp_load_head(sp, h):
                wait(sp, drive_ready, h)
                wait(sp, xc_ready, h)
                sp.wait_ge(x2_saved, h * (B * 16) + B * 16)
                sp.dma_start(xn[:, :, :, :].rearrange("p b j d -> p b (j d)"),
                             x2_d.rearrange("(h b) p x -> h p b x", b=B)[h]).then_inc(xn_in, 16)

            def sp_store(sp, h):
                for bg in range(2):
                    sp.wait_ge(out_cp_a, FIRST + h * 2 + (bg + 1))
                    sp.wait_ge(out_cp_v, FIRST + h * 2 + (bg + 1))
                    sp.dma_start(out[bg * 4:bg * 4 + 4, bass.ds(h * DH, DH), :],
                                 outs[:, bg, :, :].rearrange("p j i -> p (j i)")).then_inc(out_saved, 16)

            @block.sync
            def _(sp):
                sp.sem_inc(out_saved, FIRST_DMA)
                sp.wait_ge(pad_ready, 4)
                load_q(sp, 0, 0)
                load_k(sp, 0, 0)
                load_q(sp, 0, 1)
                sp_iteration(sp, None, 0, "first", 1)
                with sp.Fori(1, LEAD - 2) as a:
                    sp_iteration(sp, None, a, "full", a + 1)
                sp_iteration(sp, None, LEAD - 2, "full", 0)
                sp_iteration(sp, None, LEAD - 1, "full", 1, 0)

                def head(h):
                    with sp.Fori(0, B - 2) as b:
                        sp_iteration(sp, 1, h * B + b + LEAD, "full", b + 2)
                    sp_iteration(sp, 1, h * B + (B - 2 + LEAD), "full", 0)
                    sp_iteration(sp, 1, h * B + (B - 1 + LEAD), "full", 1, h + 1)
                    sp_store(sp, h)

                with sp.Fori(0, NHEAD - 2) as h:
                    head(h)
                last = NHEAD - 2
                with sp.Fori(0, B - 2) as b:
                    sp_iteration(sp, 1, b + (last * B + LEAD), "full", b + 2)
                sp_iteration(sp, 1, ELEMENTS - 1, "last")
                sp_iteration(sp, 1, ELEMENTS, "drain", None, NHEAD - 1)
                sp_store(sp, last)
                sp_store(sp, NHEAD - 1)
                sp.wait_ge(out_saved, FIRST_DMA + NHEAD * 32)

            @block.tensor
            def _(pe):
                pe.wait_ge(pad_ready, 4)

                def scores(a, t, alone):
                    wait(pe, exp_done, a * QT + t - (1 if alone else 0))
                    first = scores_bank(t, alone)
                    if t == 0:
                        pe.wait_ge(k_in, a * 80 + 80)
                        pe.wait_ge(q1_in, a * 48 + 48)
                    if t == GROUP:
                        pe.wait_ge(q2_in, a * 48 + 48)
                    for half in range(2):
                        for stack in range(2):
                            last = nc.tensor.matmul(bank[:, first + half, :], qp[:, stack, t * P:(t + 1) * P],
                                                    kp[:, stack, half * BANK:(half + 1) * BANK],
                                                    start=stack == 0, stop=stack == 1)
                    last.then_inc(s_ready, 1)

                def turn(a, t, part):
                    u = a * QT + t
                    if part == 0:
                        pe.wait_ge(exp_done, u + 1)
                        wait(pe, pt2_out, u)
                    else:
                        pe.wait_ge(pt1_out, u + 1)
                    for k in range(4):
                        j = 4 * part + k
                        last = nc.tensor.transpose(bank[:, PT_BANK, k * P:(k + 1) * P],
                                                   prob[:, t % 2, j * P:(j + 1) * P], ident[:, :])
                    last.then_inc((pt1_ready, pt2_ready)[part], 1)

                def values(a, n, piece):
                    gi = a * 2 + n
                    if piece == 0:
                        pe.wait_ge(pt1_out, gi * GROUP + GROUP)
                        pe.wait_ge(pt2_out, gi * GROUP + GROUP)
                        wait(pe, o_reduced, gi)
                        pe.wait_ge(v_in, a * 16 + 16)
                    qh, k = piece // 2, piece % 2
                    cols = slice(qh * BANK // 2, (qh + 1) * BANK // 2)
                    for g in range(G):
                        j = 2 * g + k
                        last = nc.tensor.matmul(bank[g * QUAD:g * QUAD + DH, O_BANK, cols], vh[:, j, :],
                                                prob_t[:, n, j, cols], start=k == 0, stop=k == 1)
                    if piece == 3:
                        last.then_inc(av_ready, 1)

                def turn_values(a, n):
                    gi = a * 2 + n
                    pe.wait_ge(o_out, gi + 1)
                    for k in range(GROUP):
                        last = nc.tensor.transpose(bank[:, O_BANK, k * P:(k + 1) * P], o_sb[:, k * P:(k + 1) * P],
                                                   ident[:, :])
                    last.then_inc(ot_ready, 1)

                def attention(a, mode, k, alone):
                    t, odd = k // 2, k % 2
                    prev, cur = mode != "first", mode != "drain"
                    if alone and not odd:
                        scores(a, t, alone)
                    if t < 2 and prev:
                        turn(a - 1, QT - 2 + t, odd)
                    if t >= 2 and cur:
                        turn(a, t - 2, odd)
                    if odd:
                        if cur and not alone:
                            scores(a, t, alone)
                    elif t < 6:
                        if prev:
                            for n, piece in {0: ((0, 2), (0, 3)), 1: ((0, "turn"),), 2: ((1, 0),), 3: ((1, 1),),
                                             4: ((1, 2), (1, 3)), 5: ((1, "turn"),)}[t]:
                                if piece == "turn":
                                    turn_values(a - 1, n)
                                else:
                                    values(a - 1, n, piece)
                    elif cur:
                        values(a, 0, t - 6)

                def product(half, part):
                    for c in range(JH):
                        mj = half * JH + c
                        for g in range(G):
                            w = cwh[:, part, mj, :].rearrange("p (c q n) -> p c q n", c=J, q=G)[:, :, g, :]
                            last = nc.tensor.matmul(
                                bank[g * QUAD:g * QUAD + M_COLS, MAIN_BANK, 0:J * QUAD], th16[:, part, mj, :], w,
                                start=half == 0 and part == 1 and c == 0,
                                stop=half == 1 and part == 0 and c == JH - 1, skip_group_check=True)
                    return last

                def iteration(ode, a, mode):
                    for k in range(SLOTS):
                        if ode:
                            K = (ode[0] * B + ode[1]) * SLOTS + k
                            for half in range(2):
                                pe.wait_ge(high_ready[half], K + 1)
                                product(half, 1)
                                pe.wait_ge(low_ready[half], K + 1)
                                last = product(half, 0)
                            last.then_inc(main_done, 1)
                        if mode:
                            attention(a, mode, k, not ode)

                def output(h):
                    pe.wait_ge(xo_ready, FIRST + h * DH + DH)
                    for n in range(4):
                        bg, nh = n // 2, n % 2
                        if n < 3:
                            pe.wait_ge((out_cp_a, out_cp_v)[nh], FIRST + h * 2)
                        if n == 3:
                            pe.wait_ge(out_cp_v, FIRST + h * 2 + 1)
                        for k in range(JH):
                            last = nc.tensor.transpose(
                                bank[:, OUT_BANKS[n], k * P:(k + 1) * P],
                                xo[:, nh * JH + k, 4 * bg:4 * bg + 4, :].rearrange("p b d -> p (b d)"), ident[:, :])
                        last.then_inc(out_turned, 1)

                run_engine(pe, iteration, nothing, output)

            @block.scalar
            def _(act):
                def exponent(a, t, alone):
                    u = a * QT + t
                    act.wait_ge(max_ready, u + 1)
                    if not (isinstance(u, int) and u < 2):
                        act.wait_ge(pt2_ready, u - 1)
                    first = scores_bank(t, alone)
                    nc.scalar.activation(prob[:, t % 2, :].rearrange("p (c n) -> p c n", c=2),
                                         bank[:, first:first + 2, :], ACT.Exp,
                                         bias=nmax[:, t:t + 1], scale=1.0,
                                         accum_out=rsum[:, t:t + 1]).then_inc(exp_done, 1)

                def copy_out(a, t):
                    n, q = t // GROUP, t % GROUP
                    act.wait_ge(pt2_ready, a * QT + t + 1)
                    if q == 0:
                        wait(act, av_ready, (a - 1) * 2 + n + 1)
                    nc.scalar.copy(prob_t[:, n, 4:8, q * P:(q + 1) * P],
                                   bank[:, PT_BANK, :].rearrange("p (k n) -> p k n", n=P)).then_inc(pt2_out, 1)

                def attention(a, mode, k, alone):
                    t, odd = k // 2, k % 2
                    prev, cur = mode != "first", mode != "drain"
                    if odd:
                        if t == 0 and prev:
                            exponent(a - 1, QT - 1, alone)
                        if t >= 1 and cur:
                            exponent(a, t - 1, alone)
                    else:
                        if t < 3 and prev:
                            copy_out(a - 1, QT - 3 + t)
                        if t >= 3 and cur:
                            copy_out(a, t - 3)

                def tanh_high(K):
                    for x in range(2):
                        js = slice(x * JH, (x + 1) * JH)
                        act.wait_ge(q_ready[x], K + 1)
                        nc.scalar.activation(th16[:, :, js, H_COL:H_COL + B],
                                             half_of(qs, x).unsqueeze(1).broadcast_to([P, 2, JH, B]), ACT.Tanh)\
                            .then_inc(high_ready[x], 1)
                        nc.scalar.activation(half_of(tanh, x), half_of(qs, x), ACT.Tanh)
                        act.wait_ge(high_ready[x], K + 1)
                        nc.scalar.activation(half_of(high, x), th16[:, 1, js, H_COL:H_COL + B], ACT.Copy,
                                             scale=LOW_SCALE).then_inc(tanh_ready[x], 1)

                def iteration(ode, a, mode):
                    for k in range(SLOTS):
                        if mode:
                            attention(a, mode, k, not ode)
                        if ode:
                            K = (ode[0] * B + ode[1]) * SLOTS + k
                            tanh_high(K + 1)

                def start():
                    act.sem_inc(out_cp_a, FIRST)
                    act.wait_ge(pad_ready, 4)
                    tanh_high(0)

                def begin(h):
                    act.wait_ge(xn_in, h * 16 + 16)
                    act.wait_ge(xo_ready, FIRST + h * DH)
                    nc.scalar.copy(xc[:, :, :, :], xn[:, :, :, :]).then_inc(xc_ready, 1)

                def output(h):
                    for bg in range(2):
                        act.wait_ge(out_turned, h * 4 + (2 * bg + 1))
                        if bg == 0:
                            act.wait_ge(out_saved, FIRST_DMA + h * 32)
                        nc.scalar.copy(outs[:, bg, 0:JH, :], bank[:, OUT_BANKS[2 * bg], :].rearrange("p (j i) -> p j i", i=P))\
                            .then_inc(out_cp_a, 1)

                run_engine(act, iteration, begin, output, before=start)

            @block.gpsimd
            def _(pool):
                for t in (qp, kp):
                    pool.memset(t[:, :, :], 0.0).then_inc(pad_ready, 1)
                pool.wait_ge(pad_ready, 2)
                pool.memset(qp[3 * DH:3 * DH + 3, 1, :], 1.0).then_inc(pad_ready, 1)
                pool.wait_ge(pad_ready, 3)
                pool.memset(th16[:, :, :, :], 0.0).then_inc(pad_ready, 1)
                pool.sem_inc(p_ready, FIRST)
                for tile, value in zip(consts.values(), consts):
                    pool.memset(tile[:, :, :], value).then_inc(const_ready, 1)
                pool.wait_ge(const_ready, len(consts))
                count = [0]
                start = [0]

                def link(op, dst, in0, in1, beside=None):
                    count[0] += 1
                    pool.tensor_tensor(F(dst), F(in0), F(in1), op).then_inc(pool_chain, 1)
                    if beside:
                        beside()
                    pool.wait_ge(pool_chain, start[0] + count[0])

                def drive_less_p(s, i, PP):
                    pool.tensor_tensor(F(dmp[s % 2]), drive[:, :, :, i].rearrange("p b j -> p j b"), F(PP),
                                       ALU.subtract).then_inc(dmp_ready, 1)

                def stage(K, step, s, i):
                    c = STAGE_C[s]
                    Q = q0 if s == 0 else qs
                    PP = p0 if s == 0 else ps_[(s - 1) % 2]
                    slope = racc if s == 0 else pr
                    if s == 0:
                        pool.wait_ge(p_ready, K + 1)
                    link(ALU.mult, pm, PP, consts[-BETA], beside=lambda: drive_less_p(s, i, PP))
                    if s in (0, 2):
                        link(ALU.add, p0c, p0, consts[c * EPSILON * ALPHA])
                    if s == 0:
                        pool.wait_ge(q0_ready, step + 1)
                    else:
                        for x in range(2):
                            pool.wait_ge(q_ready[x], K + 1)
                    pool.tensor_tensor(F(slope), F(pm), F(Q), ALU.add).then_inc(q_read, 1)
                    pool.wait_ge(q_read, K + 1)
                    if s < STAGES - 1:
                        link(ALU.mult, pt, slope, consts[c * EPSILON])
                        pool.tensor_tensor(F(ps_[s % 2]), F(pt), F(p0c), ALU.add).then_inc(p_ready, 1)
                        pool.wait_ge(p_ready, K + 2)
                        if s > 0:
                            link(ALU.add, racc, racc, pr)
                            link(ALU.add, racc, racc, pr)
                    else:
                        link(ALU.add, racc, racc, pr)
                        link(ALU.mult, pt, racc, consts[c * EPSILON])
                        pool.tensor_tensor(F(pn), F(pt), F(p0c), ALU.add).then_inc(pn_ready, 1)

                def iteration(ode, a, mode):
                    it = ode[0] * B + ode[1]
                    count[0] = 0
                    start[0] = it * POOL_PER_ITERATION
                    pool.wait_ge(drive_ready, ode[0] + 1)
                    for i in range(STEPS):
                        for s in range(STAGES):
                            stage(it * SLOTS + (i * STAGES + s), it * STEPS + i, s, ode[1] * STEPS + i)
                    assert count[0] == POOL_PER_ITERATION, count[0]

                run_engine(pool, iteration, nothing, nothing, attends=False)

            @block.vector
            def _(dve):
                count = [0]
                start = [0]

                def made(ins):
                    count[0] += 1
                    ins.then_inc(chain, 1)
                    return start[0] + count[0]

                def row_max(a, t, alone):
                    first = scores_bank(t, alone)
                    dve.wait_ge(s_ready, a * QT + t + 1)
                    dve.tensor_reduce(nmax[:, t:t + 1], bank[:, first:first + 2, :], AX.XY, ALU.max,
                                      negate=True).then_inc(max_ready, 1)

                def copy_out(a, t):
                    n, q = t // GROUP, t % GROUP
                    dve.wait_ge(pt1_ready, a * QT + t + 1)
                    if q == 0:
                        wait(dve, av_ready, (a - 1) * 2 + n + 1)
                    dve.tensor_copy(prob_t[:, n, 0:4, q * P:(q + 1) * P],
                                    bank[:, PT_BANK, :].rearrange("p (k n) -> p k n", n=P)).then_inc(pt1_out, 1)

                def invert(a, n):
                    dve.wait_ge(exp_done, a * QT + GROUP * (n + 1))
                    g = slice(GROUP * n, GROUP * (n + 1))
                    dve.reciprocal(rinv[:, g], rsum[:, g]).then_inc(inv_ready, 1)

                def copy_values(a, n):
                    dve.wait_ge(av_ready, a * 2 + n + 1)
                    dve.tensor_copy(o_sb[:, :], bank[:, O_BANK, :]).then_inc(o_out, 1)

                def normalise(a, n):
                    gi = a * 2 + n
                    g = slice(GROUP * n, GROUP * (n + 1))
                    dve.wait_ge(ot_ready, gi + 1)
                    dve.tensor_reduce(o_red[:, :, :], bank[:, O_BANK, :].rearrange("p (q g d) -> p q d g", q=GROUP, g=G),
                                      AX.X, ALU.add).then_inc(o_reduced, 1)
                    dve.wait_ge(o_reduced, gi + 1)
                    dve.wait_ge(inv_ready, gi + 1)
                    dve.tensor_tensor(o_nrm[:, :, :], o_red[:, :, :],
                                      rinv[:, g].unsqueeze(2).broadcast_to([P, GROUP, DH]), ALU.mult)\
                        .then_inc(o_scaled, 1)

                def add_to_x(a, n):
                    g = slice(GROUP * n, GROUP * (n + 1))
                    dve.wait_ge(o_scaled, a * 2 + n + 1)
                    dve.wait_ge(xt_in, a * 16 + 16)
                    if n == 0:
                        wait(dve, x2_saved, a * 16)
                    dve.tensor_tensor(x2[:, g, :], xt[:, g, :], o_nrm[:, :, :], ALU.add).then_inc(x2_ready, 1)

                def attention(a, mode, k, alone):
                    t, odd = k // 2, k % 2
                    prev, cur = mode != "first", mode != "drain"
                    if not odd:
                        if t == 0 and prev:
                            row_max(a - 1, QT - 1, alone)
                        if t >= 1 and cur:
                            row_max(a, t - 1, alone)
                        if t == 1 and prev:
                            invert(a - 1, 1)
                        if t in (2, 6) and prev:
                            add_to_x(a - 1, t // 4)
                        if t == 6 and cur:
                            invert(a, 0)
                    else:
                        if t < 2 and prev:
                            copy_out(a - 1, QT - 2 + t)
                        if t >= 2 and cur:
                            copy_out(a, t - 2)
                        if prev and t in (1, 5):
                            normalise(a - 1, t // 4)
                        if prev and t in (0, 4):
                            copy_values(a - 1, t // 4)

                def low_part(x, K):
                    part = th16[:, 0, x * JH:(x + 1) * JH, :]
                    dve.wait_ge(tanh_ready[x], K + 1)
                    dve.scalar_tensor_tensor(part[:, :, L_COL:L_COL + B], half_of(tanh, x), LOW_SCALE,
                                             half_of(high, x), ALU.mult, ALU.subtract)\
                        .then_inc(low_ready[x], 1)

                def stage(K, k, i, attend):
                    s = k % STAGES
                    c = STAGE_C[s]
                    Q = q0 if s == 0 else qs
                    dve.wait_ge(sq_ready, K + 1)
                    n_w3 = made(dve.scalar_tensor_tensor(F(w3), F(sq), -3.0, F(Q), ALU.add, ALU.mult))
                    dve.wait_ge(dmp_ready, K + 1)
                    dve.wait_ge(chain, n_w3)
                    n_ff = made(dve.scalar_tensor_tensor(F(ff), F(w3), -1.0 / 3.0, F(dmp[k % 2]), ALU.mult, ALU.add))
                    if k > 0:
                        low_part(1, K)
                    dve.wait_ge(chain, n_ff)
                    ff_all = ff
                    if s == STAGES - 1:
                        n_all = made(dve.tensor_tensor(F(ffa), F(ff), F(acc), ALU.add))
                        dve.wait_ge(chain, n_all)
                        ff_all = ffa
                    n_base = made(dve.scalar_tensor_tensor(F(base), F(ff_all), c, F(q0), ALU.mult, ALU.add))
                    attend()
                    dve.wait_ge(chain, n_base)
                    dve.wait_ge(q_read, K + 1)
                    dve.wait_ge(main_done, K + 1)
                    for x in range(2):
                        cols = slice(x * JH * QUAD, (x + 1) * JH * QUAD)
                        dve.transpose(half_of(sums, x).rearrange("p j m -> p (j m)"), bank[:, MAIN_BANK, cols])\
                            .then_inc(sums_turned, 1)
                    for x in range(2):
                        dve.wait_ge(sums_turned, K * 2 + (x + 1))
                        dve.scalar_tensor_tensor(half_of(isum, x), half_of(sums, x)[:, :, L_COL:L_COL + B],
                                                 1.0 / LOW_SCALE, half_of(sums, x)[:, :, H_COL:H_COL + B],
                                                 ALU.mult, ALU.add).then_inc(isum_ready, 1)
                    for x in range(2):
                        dve.wait_ge(isum_ready, K * 2 + (x + 1))
                        dve.scalar_tensor_tensor(half_of(qs, x), half_of(isum, x), isum_c[:, s:s + 1],
                                                 half_of(base, x), ALU.mult, ALU.add).then_inc(q_ready[x], 1)
                    if s == STAGES - 1:
                        dve.wait_ge(q_ready[1], K + 2)
                        dve.tensor_scalar(F(q0), F(qs), -CLAMP, CLAMP, ALU.max, ALU.min).then_inc(q0_ready, 1)
                        return
                    n_kk = made(dve.scalar_tensor_tensor(F(kk if s else acc), F(isum), unscale[:, 0:1], F(ff),
                                                         ALU.mult, ALU.add))
                    dve.wait_ge(q_ready[1], K + 2)
                    dve.tensor_tensor(F(sq), F(qs), F(qs), ALU.mult).then_inc(sq_ready, 1)
                    if s > 0:
                        dve.wait_ge(chain, n_kk)
                        made(dve.scalar_tensor_tensor(F(acc), F(kk), 2.0, F(acc), ALU.mult, ALU.add))

                def iteration(ode, a, mode):
                    if ode:
                        h, b = ode
                        it = h * B + b
                        count[0] = 0
                        start[0] = it * CHAIN_PER_ITERATION
                    for k in range(SLOTS):
                        attend = lambda: attention(a, mode, k, not ode) if mode else None
                        if not ode:
                            attend()
                            continue
                        K = it * SLOTS + k
                        step = it * STEPS + k // STAGES
                        i = b * STEPS + k // STAGES
                        stage(K, k, i, attend)
                        if k % STAGES == STAGES - 1:
                            dve.wait_ge(pn_ready, step + 1)
                            dve.tensor_scalar(F(p0), F(pn), -CLAMP, CLAMP, ALU.max, ALU.min).then_inc(p_ready, 1)
                            dve.wait_ge(q0_ready, step + 2)
                            dve.tensor_tensor(F(sq), F(q0), F(q0), ALU.mult).then_inc(sq_ready, 1)
                        low_part(0, K + 1)
                        if k % STAGES == STAGES - 1:
                            if k == STAGES - 1:
                                dve.wait_ge(xc_ready, h + 1)
                            dve.tensor_tensor(xo[:, :, :, i], xc[:, :, :, i].rearrange("p b j -> p j b"), F(q0),
                                              ALU.add).then_inc(xo_ready, 1)
                        if k == SLOTS - 1:
                            low_part(1, K + 1)
                    if ode:
                        assert count[0] == CHAIN_PER_ITERATION, count[0]

                def start_ode():
                    dve.sem_inc(q0_ready, FIRST)
                    dve.sem_inc(xo_ready, FIRST)
                    dve.sem_inc(out_cp_v, FIRST)
                    for x in range(2):
                        dve.tensor_copy(half_of(qs, x), half_of(q0, x)).then_inc(q_ready[x], 1)
                    dve.wait_ge(pad_ready, 4)
                    dve.tensor_tensor(F(sq), F(q0), F(q0), ALU.mult).then_inc(sq_ready, 1)
                    for x in range(2):
                        low_part(x, 0)

                def begin(h):
                    dve.wait_ge(xn_in, h * 16 + 16)
                    dve.tensor_tensor(drive[:, :, :, :], xn[:, :, :, :],
                                      bias_col[:, :].unsqueeze(1).unsqueeze(3).broadcast_to([P, B, J, DH]),
                                      ALU.add).then_inc(drive_ready, 1)

                def output(h):
                    for bg in range(2):
                        dve.wait_ge(out_turned, h * 4 + (2 * bg + 2))
                        if bg == 0:
                            dve.wait_ge(out_saved, FIRST_DMA + h * 32)
                        dve.tensor_copy(outs[:, bg, JH:J, :], bank[:, OUT_BANKS[2 * bg + 1], :].rearrange("p (j i) -> p j i", i=P))\
                            .then_inc(out_cp_v, 1)

                run_engine(dve, iteration, begin, output, before=start_ode, begin_first=True, unroll=2)


POOL_PER_ITERATION = 4 * (3 + 4 + 5 + 3)
CHAIN_PER_ITERATION = 4 * (4 + 5 + 5 + 4)


_INS = ["x", "cond_2048", "L0_cond_Wq", "L0_cond_Wk", "L0_cond_Wv", "L0_cond_b", "L1_cond_coupling", "L1_cond_bias"]
_OUTS = [((8, 512, 1024), "float32")]


def kernel(**inputs):
    import numpy as _np
    import concourse.bacc as _bacc
    from concourse import mybir as _mybir
    from concourse.bass_utils import run_bass_kernel_spmd as _run

    nc = _bacc.Bacc("TRN2", target_bir_lowering=False, num_devices=1)
    arrays, args = {}, []
    for name in _INS:
        a = _np.ascontiguousarray(inputs[name])
        arrays[f"in_{name}_dram"] = a
        args.append(nc.dram_tensor(f"in_{name}_dram", a.shape, _mybir.dt.from_np(a.dtype), kind="ExternalInput").ap())
    for i, (shape, dtype) in enumerate(_OUTS):
        dt = _mybir.dt.from_np(_np.dtype(dtype))
        args.append(nc.dram_tensor(f"out_{i}_dram", shape, dt, kind="ExternalOutput").ap())
    build_program(nc, *args)
    r = _run(nc, [arrays], core_ids=[0])
    return r.results[0]["out_0_dram"]
```
